# Optimizing a Trainium2 kernel written in Bass

```python
import numpy as np
import jax
import jax.numpy as jnp

def _softmax(x, axis=-1):
    return jax.nn.softmax(x, axis=axis)

def _gelu(x):
    return jax.nn.gelu(x, approximate=True)

def _silu(x):
    return jax.nn.silu(x)

def _sigmoid(x):
    return jax.nn.sigmoid(x)

def _layernorm(x, axis=-1, eps=1e-05):
    m = jnp.mean(x, axis=axis, keepdims=True)
    v = jnp.var(x, axis=axis, keepdims=True)
    return (x - m) / jnp.sqrt(v + eps)

def _scatter_add(tgt, idx, src, axis=0):
    return tgt.at[idx].add(src)

def _segment_sum(src, seg, n):
    return jax.ops.segment_sum(src, seg, n)
kernel_name = 'mk_seq_postln_d1_jaxref_r8_98189b'

def setup_inputs(seed: int=0):
    np.random.seed(seed)
    _w = jnp.asarray

    def _L0_attn_setup():
        import jax, jax.numpy as jnp
        import numpy as np
        B, S, DIM, H = (2, 256, 128, 16)
        D = DIM // H

        def _xavier(key, shape):
            a = float(np.sqrt(6.0 / (shape[0] + shape[1])))
            return jax.random.uniform(key, shape, minval=-a, maxval=a, dtype=jnp.float32)

        def _split_heads(t):
            b, s, _ = t.shape
            return t.reshape(b, s, H, D).transpose(0, 2, 1, 3).reshape(b * H, s, D)
        key = jax.random.key(seed)
        ks = jax.random.split(key, 8)
        x = jax.random.normal(ks[0], (B, S, DIM), dtype=jnp.float32)
        Wq = _xavier(ks[1], (DIM, DIM))
        Wk = _xavier(ks[2], (DIM, DIM))
        Wv = _xavier(ks[3], (DIM, DIM))
        Wo = _xavier(ks[4], (DIM, DIM))
        bq = jax.random.normal(ks[5], (DIM,), dtype=jnp.float32) * 0.02
        bk = jax.random.normal(ks[6], (DIM,), dtype=jnp.float32) * 0.02
        bv = jax.random.normal(ks[7], (DIM,), dtype=jnp.float32) * 0.02
        bo = jnp.zeros((DIM,), dtype=jnp.float32)
        return {'x': x, 'Wq': Wq, 'bq': bq, 'Wk': Wk, 'bk': bk, 'Wv': Wv, 'bv': bv, 'Wo': Wo, 'bo': bo}
    _L0_attn_in = _L0_attn_setup()

    def _L0_ffn_setup():
        import jax, jax.numpy as jnp
        import numpy as np
        N_EXPERTS = 32
        TOP_K = 8
        N_GROUP = 4
        TOPK_GROUP = 2
        ROUTED_SCALING = 2.5

        def _gate(x, gate_w, gate_bias):
            T, E = (x.shape[0], gate_w.shape[0])
            logits = jnp.einsum('th,eh->te', x, gate_w)
            scores = jax.nn.sigmoid(logits)
            scores_choice = scores + gate_bias[None, :]
            grp = scores_choice.reshape(T, N_GROUP, E // N_GROUP)
            top2, _ = jax.lax.top_k(grp, 2)
            group_scores = top2.sum(-1)
            _, grp_idx = jax.lax.top_k(group_scores, TOPK_GROUP)
            group_mask = jax.nn.one_hot(grp_idx, N_GROUP, dtype=scores.dtype).sum(1)
            expert_mask = jnp.repeat(group_mask, E // N_GROUP, axis=1)
            masked = jnp.where(expert_mask > 0, scores_choice, 0.0)
            _, topk_idx = jax.lax.top_k(masked, TOP_K)
            topk_w = jnp.take_along_axis(scores, topk_idx, axis=1)
            topk_w = topk_w / (topk_w.sum(-1, keepdims=True) + 1e-20)
            topk_w = topk_w * ROUTED_SCALING
            return (topk_idx, topk_w)

        def _mlp(x, wg, wu, wd):
            return jnp.einsum('...i,hi->...h', jax.nn.silu(jnp.einsum('...h,ih->...i', x, wg)) * jnp.einsum('...h,ih->...i', x, wu), wd)
        key = jax.random.key(seed)
        ks = jax.random.split(key, 9)
        B, S, H, I = (2, 64, 128, 64)
        w = 0.02
        return {'hidden_states': jax.random.normal(ks[0], (B, S, H), jnp.float32), 'gate_w': jax.random.normal(ks[1], (N_EXPERTS, H), jnp.float32) * w, 'gate_bias': jax.random.normal(ks[2], (N_EXPERTS,), jnp.float32) * w, 'expert_gate': jax.random.normal(ks[3], (N_EXPERTS, I, H), jnp.float32) * w, 'expert_up': jax.random.normal(ks[4], (N_EXPERTS, I, H), jnp.float32) * w, 'expert_down': jax.random.normal(ks[5], (N_EXPERTS, H, I), jnp.float32) * w, 'shared_gate': jax.random.normal(ks[6], (2 * I, H), jnp.float32) * w, 'shared_up': jax.random.normal(ks[7], (2 * I, H), jnp.float32) * w, 'shared_down': jax.random.normal(ks[8], (H, 2 * I), jnp.float32) * w}
    _L0_ffn_in = _L0_ffn_setup()
    _d = {'L0_attn_x': _L0_attn_in['x'], 'L0_attn_Wq': _L0_attn_in['Wq'], 'L0_attn_bq': _L0_attn_in['bq'], 'L0_attn_Wk': _L0_attn_in['Wk'], 'L0_attn_bk': _L0_attn_in['bk'], 'L0_attn_Wv': _L0_attn_in['Wv'], 'L0_attn_bv': _L0_attn_in['bv'], 'L0_attn_Wo': _L0_attn_in['Wo'], 'L0_attn_bo': _L0_attn_in['bo'], 'L0_ffn_gate_w': _L0_ffn_in['gate_w'], 'L0_ffn_gate_bias': _L0_ffn_in['gate_bias'], 'L0_ffn_expert_gate': _L0_ffn_in['expert_gate'], 'L0_ffn_expert_up': _L0_ffn_in['expert_up'], 'L0_ffn_expert_down': _L0_ffn_in['expert_down'], 'L0_ffn_shared_gate': _L0_ffn_in['shared_gate'], 'L0_ffn_shared_up': _L0_ffn_in['shared_up'], 'L0_ffn_shared_down': _L0_ffn_in['shared_down']}
    _x0 = _d['L0_attn_x']
    _d['L0_attn_x'] = jax.random.normal(jax.random.fold_in(jax.random.key(seed), 1), (16, 256, 128), dtype=_x0.dtype)
    del _x0
    return _d

def reference(L0_attn_x, L0_attn_Wq, L0_attn_bq, L0_attn_Wk, L0_attn_bk, L0_attn_Wv, L0_attn_bv, L0_attn_Wo, L0_attn_bo, L0_ffn_gate_w, L0_ffn_gate_bias, L0_ffn_expert_gate, L0_ffn_expert_up, L0_ffn_expert_down, L0_ffn_shared_gate, L0_ffn_shared_up, L0_ffn_shared_down):

    def _L0_attn_ref(x, Wq, bq, Wk, bk, Wv, bv, Wo, bo):
        import jax, jax.numpy as jnp
        import numpy as np
        B, S, DIM, H = (2, 256, 128, 16)
        D = DIM // H

        def _xavier(key, shape):
            a = float(np.sqrt(6.0 / (shape[0] + shape[1])))
            return jax.random.uniform(key, shape, minval=-a, maxval=a, dtype=jnp.float32)

        def _split_heads(t):
            b, s, _ = t.shape
            return t.reshape(b, s, H, D).transpose(0, 2, 1, 3).reshape(b * H, s, D)
        b, s, _ = x.shape
        q = _split_heads(x @ Wq.T + bq)
        k = _split_heads(x @ Wk.T + bk)
        v = _split_heads(x @ Wv.T + bv)
        q = jnp.exp(q)
        k = jnp.exp(k)
        kv = jnp.cumsum(k[:, :, :, None] * v[:, :, None, :], axis=1)
        k1 = jnp.cumsum(k, axis=1)
        num = jnp.einsum('zsD,zsDd->zsd', q, kv)
        den = jnp.sum(q * k1, axis=-1, keepdims=True)
        out = num / den
        out = out.reshape(b, H, s, D).transpose(0, 2, 1, 3).reshape(b, s, DIM)
        return out @ Wo.T + bo

    def _L0_ffn_ref(hidden_states, gate_w, gate_bias, expert_gate, expert_up, expert_down, shared_gate, shared_up, shared_down):
        import jax, jax.numpy as jnp
        import numpy as np
        N_EXPERTS = 32
        TOP_K = 8
        N_GROUP = 4
        TOPK_GROUP = 2
        ROUTED_SCALING = 2.5

        def _gate(x, gate_w, gate_bias):
            T, E = (x.shape[0], gate_w.shape[0])
            logits = jnp.einsum('th,eh->te', x, gate_w)
            scores = jax.nn.sigmoid(logits)
            scores_choice = scores + gate_bias[None, :]
            grp = scores_choice.reshape(T, N_GROUP, E // N_GROUP)
            top2, _ = jax.lax.top_k(grp, 2)
            group_scores = top2.sum(-1)
            _, grp_idx = jax.lax.top_k(group_scores, TOPK_GROUP)
            group_mask = jax.nn.one_hot(grp_idx, N_GROUP, dtype=scores.dtype).sum(1)
            expert_mask = jnp.repeat(group_mask, E // N_GROUP, axis=1)
            masked = jnp.where(expert_mask > 0, scores_choice, 0.0)
            _, topk_idx = jax.lax.top_k(masked, TOP_K)
            topk_w = jnp.take_along_axis(scores, topk_idx, axis=1)
            topk_w = topk_w / (topk_w.sum(-1, keepdims=True) + 1e-20)
            topk_w = topk_w * ROUTED_SCALING
            return (topk_idx, topk_w)

        def _mlp(x, wg, wu, wd):
            return jnp.einsum('...i,hi->...h', jax.nn.silu(jnp.einsum('...h,ih->...i', x, wg)) * jnp.einsum('...h,ih->...i', x, wu), wd)
        orig_shape = hidden_states.shape
        H = orig_shape[-1]
        residuals = hidden_states
        x = hidden_states.reshape(-1, H)
        topk_idx, topk_w = _gate(x, gate_w, gate_bias)
        g = jnp.einsum('th,eih->eti', x, expert_gate)
        u = jnp.einsum('th,eih->eti', x, expert_up)
        outs = jnp.einsum('eti,ehi->eth', jax.nn.silu(g) * u, expert_down)
        outs_t = jnp.transpose(outs, (1, 0, 2))
        gathered = jnp.take_along_axis(outs_t, topk_idx[:, :, None], axis=1)
        final = (gathered * topk_w[:, :, None]).sum(1)
        shared = _mlp(residuals, shared_gate, shared_up, shared_down)
        return final.reshape(orig_shape) + shared
    x = L0_attn_x
    x = _layernorm(x + _L0_attn_ref(x, L0_attn_Wq, L0_attn_bq, L0_attn_Wk, L0_attn_bk, L0_attn_Wv, L0_attn_bv, L0_attn_Wo, L0_attn_bo), axis=-1)
    x = _layernorm(x + _L0_ffn_ref(x, L0_ffn_gate_w, L0_ffn_gate_bias, L0_ffn_expert_gate, L0_ffn_expert_up, L0_ffn_expert_down, L0_ffn_shared_gate, L0_ffn_shared_up, L0_ffn_shared_down), axis=-1)
    return x

_drawn_inputs = setup_inputs


def setup_inputs(seed=0):
    import zlib

    import numpy as np

    out = dict(_drawn_inputs(seed))
    spreads = {'L0_attn_bo': (0.0, 0.1)}
    factors = {'L0_attn_bq': 8.0,
     'L0_attn_bk': 8.0,
     'L0_attn_bv': 2.929,
     'L0_ffn_gate_w': 8.0,
     'L0_ffn_gate_bias': 8.0,
     'L0_ffn_expert_gate': 8.0,
     'L0_ffn_expert_up': 8.0,
     'L0_ffn_expert_down': 8.0,
     'L0_ffn_shared_gate': 8.0,
     'L0_ffn_shared_up': 8.0,
     'L0_ffn_shared_down': 8.0}
    for name, (base, spread) in spreads.items():
        noise = np.random.default_rng([zlib.crc32(name.encode()), seed]).standard_normal(out[name].shape)
        drawn = base * np.exp(spread * noise) if base else spread * noise
        out[name] = jnp.asarray(drawn.astype(out[name].dtype))
    for name, factor in factors.items():
        out[name] = (out[name] * factor).astype(out[name].dtype)
    return out
```

```python
import concourse.bass as bass
from concourse import mybir
from contextlib import ExitStack

TOKENS, DIM = 4096, 128
SEQ, HEADS, HEAD_DIM = 256, 16, 8
EXPERTS, INTER = 32, 64
EXPERT_GROUPS, TOP_K, TOP_GROUPS = 4, 8, 2
ROUTED_SCALING = 2.5
LN_EPS = 1e-5

GROUP = 512
GROUPS = TOKENS // GROUP
TILES = GROUP // 128
SEQS = GROUP // SEQ
CHUNK = 64
CHUNKS = SEQ // CHUNK
QUADS = HEADS // 4
PARTS = 3
STACK = PARTS * 32
BLOCKS = EXPERTS * INTER // 128 + 1
ROUTED = BLOCKS - 1
PIECES = 4
PIECE = ROUTED // PIECES
SLOTS = BLOCKS
HEAD_SLOTS = 4
LAG = 2
STACK_LOADS = PARTS * (4 + 2)

CONST_COLS = {"ident": 128, "block": 128, "tri": 64, "half": 16, "ones": 16, "lower": 16}


def attention_moe_kernel(nc, xT_d, x_d, attn_w_d, attn_cols_d, bo_d, gate_bias_d,
                         up_d, down_d, const_d, out_d):
    F32, F32R = mybir.dt.float32, mybir.dt.float32r
    ALU = mybir.AluOpType
    ACT = mybir.ActivationFunctionType
    AX = mybir.AxisListType

    ctx = ExitStack()
    with ctx:
        def sb(name, shape, dt=F32):
            return ctx.enter_context(nc.sbuf_tensor(name, shape, dt))

        def sem(name):
            return ctx.enter_context(nc.semaphore(name))

        const = sb("const", [128, sum(CONST_COLS.values())])
        at, views = 0, {}
        for name, n in CONST_COLS.items():
            views[name] = const[:, at:at + n]
            at += n
        ident, block_mask, tri = views["ident"], views["block"], views["tri"]
        half_mask, head_ones, lower = views["half"], views["ones"], views["lower"]
        attn_w = sb("attn_w", [128, 4 * DIM + EXPERTS])
        wqT, wkT, wvT, woT = (attn_w[:, i * DIM:(i + 1) * DIM] for i in range(4))
        gate_wT = attn_w[:, 4 * DIM:4 * DIM + EXPERTS]
        attn_cols = sb("attn_cols", [128, 3])
        row_bias = sb("row_bias", [128, DIM])
        gate_bias = sb("gate_bias", [128, EXPERTS])
        bv_wide = sb("bv_wide", [128, 128])
        gate_hi = sb("gate_hi", [128, BLOCKS * 128], F32R)
        gate_lo = sb("gate_lo", [128, BLOCKS * 128], F32R)
        up_hi = sb("up_hi", [128, BLOCKS * 128], F32R)
        up_lo = sb("up_lo", [128, BLOCKS * 128], F32R)
        down_w = sb("down_w", [128, BLOCKS * 128])
        neg_half = sb("neg_half", [128, TILES])

        xT = sb("xT", [128, GROUP])
        qT, kT = sb("qT", [128, GROUP]), sb("kT", [128, GROUP])
        q_hi, q_lo = sb("q_hi", [128, GROUP], F32R), sb("q_lo", [128, GROUP], F32R)
        k_hi, k_lo = sb("k_hi", [128, GROUP], F32R), sb("k_lo", [128, GROUP], F32R)
        k_sum = sb("k_sum", [128, GROUP])
        k_stack = sb("k_stack", [STACK, QUADS, SEQS * CHUNKS, 2, CHUNK], F32R)
        q_stack = sb("q_stack", [STACK, QUADS, 2, GROUP], F32R)
        v_pair = sb("v_pair", [128, SEQS * CHUNKS * QUADS, 4, 16])
        k_twice = sb("k_twice", [128, CHUNKS - 1, 128])
        kv_blocks = sb("kv_blocks", [128, SEQS, CHUNKS - 1, 128])

        probs = sb("probs", [128, SEQS, QUADS, CHUNKS, 2, CHUNK])
        inv_den = sb("inv_den", [128, TILES * HEADS])
        inv_wide = sb("inv_wide", [128, TILES * HEADS, HEAD_DIM])
        inv_denT = sb("inv_denT", [128, GROUP])
        attnT = sb("attnT", [128, GROUP])
        x_tok = sb("x_tok", [128, TILES, DIM])
        resid = sb("resid", [128, TILES, DIM])
        stats = sb("stats", [128, TILES, 6])
        mean_var = sb("mean_var", [128, TILES, 2])
        var1, rstd1 = sb("var1", [128, TILES]), sb("rstd1", [128, TILES])
        x1 = [sb(f"x1_{u}", [128, TILES, DIM]) for u in range(2)]
        x1T = sb("x1T", [128, GROUP])
        x1_hi = [sb(f"x1_hi{u}", [128, GROUP], F32R) for u in range(2)]
        x1_lo = [sb(f"x1_lo{u}", [128, GROUP], F32R) for u in range(2)]
        NE = TILES * EXPERTS
        NG = TILES * EXPERT_GROUPS
        exp_neg = sb("exp_neg", [128, NE])
        score = sb("score", [128, NE])
        choice = sb("choice", [128, NE])
        top_of_group = sb("top_of_group", [128, NG, 8])
        group_score = sb("group_score", [128, NG])
        greater = sb("greater", [128, NG, EXPERT_GROUPS])
        equal = sb("equal", [128, NG, EXPERT_GROUPS])
        group_rank = sb("group_rank", [128, NG])
        masked = sb("masked", [128, NE])
        top_vals = sb("top_vals", [128, TILES, 8])
        replaced = sb("replaced", [128, NE])
        weight_sum = sb("weight_sum", [128, TILES])
        weight = sb("weight", [128, NE])
        weightT = sb("weightT", [EXPERTS, GROUP])

        weight_wide = sb("weight_wide", [128, ROUTED, GROUP])
        silu = [sb(f"silu{i}", [128, GROUP]) for i in range(2)]
        gated = [sb(f"gated{i}", [128, GROUP]) for i in range(3)]
        hidden = [sb(f"hidden{i}", [128, GROUP]) for i in range(3)]
        yT = sb("yT", [128, GROUP])
        stats2 = sb("stats2", [128, TILES, 6])
        mean_var2 = sb("mean_var2", [128, TILES, 2])
        var2, rstd2 = sb("var2", [128, TILES]), sb("rstd2", [128, TILES])
        out_sb = sb("out_sb", [128, TILES, DIM])
        up_raw = weight_wide[:, :, :].rearrange("p b t -> p (b t)")[:, 0:2 * BLOCKS * 128]

        q_hi_d, q_lo_d, k_hi_d, k_lo_d = (
            nc.dram_tensor(n, (32, QUADS, GROUP), F32).ap() for n in ("q_hi_d", "q_lo_d", "k_hi_d", "k_lo_d"))
        weight_d = nc.dram_tensor("weight_d", (2, EXPERTS, GROUP), F32).ap()

        banks = [ctx.enter_context(nc.psum_tensor(f"bank{i}", [128, 512], F32)) for i in range(8)]
        up_banks = banks[0:3]
        y_bank = banks[3]
        mid_banks = banks[4:6]
        work_bank = banks[6]
        o_bank = banks[7]

        apart, const_loaded, zeroed, w_attn_loaded = (sem(n) for n in ("apart", "const_loaded", "zeroed", "w_attn_loaded"))
        up_loaded, down_loaded, split_done, setup_chain = (sem(n) for n in ("up_loaded", "down_loaded", "split_done", "setup_chain"))
        bias_mm, bias_done, xT_loaded, q_proj = (sem(n) for n in ("bias_mm", "bias_done", "xT_loaded", "q_proj"))
        q_exp, q_hi_done, q_lo_done, k_proj = (sem(n) for n in ("q_exp", "q_hi_done", "q_lo_done", "k_proj"))
        k_exp, k_hi_done, k_lo_done, scratch_written = (sem(n) for n in ("k_exp", "k_hi_done", "k_lo_done", "scratch_written"))
        stack_loaded, v_proj, v_masked, kT_turned = (sem(n) for n in ("stack_loaded", "v_proj", "v_masked", "kT_turned"))
        kT_copied, kv_ready, kv_masked, k_scanned = (sem(n) for n in ("kT_copied", "kv_ready", "kv_masked", "k_scanned"))
        qk_sum_done, scores_ready, probs_done, o_ready = (sem(n) for n in ("qk_sum_done", "scores_ready", "probs_done", "o_ready"))
        den_ready, inv_done, inv_widened, inv_turned = (sem(n) for n in ("den_ready", "inv_done", "inv_widened", "inv_turned"))
        inv_copied, attn_done, proj_ready, x_tok_loaded = (sem(n) for n in ("inv_copied", "attn_done", "proj_ready", "x_tok_loaded"))
        x_bias_done, resid_done, ln_chain, var1_done = (sem(n) for n in ("x_bias_done", "resid_done", "ln_chain", "var1_done"))
        rstd1_done, x1_done, x1_turned, x1T_copied = (sem(n) for n in ("rstd1_done", "x1_done", "x1_turned", "x1T_copied"))
        x1_hi_done, x1_lo_done, gate_ready, gate_exp = (sem(n) for n in ("x1_hi_done", "x1_lo_done", "gate_ready", "gate_exp"))
        route_chain, weight_done, weight_turned, weightT_copied = (sem(n) for n in ("route_chain", "weight_done", "weight_turned", "weightT_copied"))
        weight_written, g_ready, u_ready, silu_done = (sem(n) for n in ("weight_written", "g_ready", "u_ready", "silu_done"))
        gated_done, hidden_done, down_done, y_copied = (sem(n) for n in ("gated_done", "hidden_done", "down_done", "y_copied"))
        y_turned, resid2_done, ln2_chain, var2_done = (sem(n) for n in ("y_turned", "resid2_done", "ln2_chain", "var2_done"))
        rstd2_done, out_done, out_stored = (sem(n) for n in ("rstd2_done", "out_done", "out_stored"))
        wide_loaded = [sem(f"wide_loaded{p}") for p in range(PIECES)]

        def reached(count):
            return max(count, 0) if isinstance(count, int) else count


        def schedule(slot, eng):
            def run(slots, g, u, **what):
                for n in slots:
                    slot(n, g, u, **what)
            every, head, rest = range(SLOTS), range(HEAD_SLOTS), range(HEAD_SLOTS, SLOTS)
            run(every, -2, 0, ffn=False, mid=False, front=True, tail=False)
            run(every, -1, 1, ffn=False, mid=True, front=True, tail=False)
            run(head, 0, 0, ffn=True, mid=True, front=True, tail=False)
            with eng.Fori(0, (GROUPS - 2) // 2) as pair:
                for u in range(2):
                    g = pair * 2 + u
                    run(rest, g, u, ffn=True, mid=True, front=True, tail=False)
                    run(head, g + 1, 1 - u, ffn=True, mid=True, front=True, tail=True)
            last = GROUPS - 1
            run(rest, last - 1, 0, ffn=True, mid=True, front=False, tail=False)
            run(head, last, 1, ffn=True, mid=False, front=False, tail=True)
            run(rest, last, 1, ffn=True, mid=False, front=False, tail=False)
            run(head, last + 1, 0, ffn=False, mid=False, front=False, tail=True)

        block = ctx.enter_context(nc.Block())

        @block.sync
        def _(sp):
            sp.dma_start(attn_w[:, :], attn_w_d).then_inc(w_attn_loaded, 16)
            sp.dma_start(attn_cols[:, :], attn_cols_d).then_inc(w_attn_loaded, 16)
            sp.dma_start(const[:, :], const_d).then_inc(const_loaded, 16)
            sp.dma_start(row_bias[:, :], bo_d.partition_broadcast(128)).then_inc(const_loaded, 16)
            sp.dma_start(gate_bias[:, :], gate_bias_d.partition_broadcast(128)).then_inc(const_loaded, 16)

            def address(value):
                return value if isinstance(value, int) else sp.snap(value)

            def slot(n, g, u, ffn, mid, front, tail):
                m, f = g + 1, g + 2
                if front and n == 4:
                    at = address(f * GROUP)
                    sp.wait_ge(v_proj, reached(SEQS * f))
                    sp.sem_inc(apart, 1)
                    sp.dma_start(xT[:, :], xT_d[:, bass.ds(at, GROUP)]).then_inc(xT_loaded, 16)
                if mid and n == 4:
                    at = address(m * GROUP)
                    sp.wait_ge(x_bias_done, reached(m))
                    sp.sem_inc(apart, 1)
                    sp.dma_start(x_tok[:, :, :], x_d[bass.ds(at, GROUP), :].rearrange("(a p) c -> p a c", p=128)
                                 ).then_inc(x_tok_loaded, 16)
                if isinstance(g, int) and g == -2 and n == 4:
                    sp.dma_start(up_raw, up_d).then_inc(up_loaded, 16)
                    sp.dma_start(down_w[:, :], down_d).then_inc(down_loaded, 16)
                if tail and n == 3:
                    t = g - 1
                    at = address(t * GROUP)
                    sp.wait_ge(out_done, reached(t + 1))
                    sp.sem_inc(apart, 1)
                    sp.dma_start(out_d[bass.ds(at, GROUP), :].rearrange("(a p) c -> p a c", p=128),
                                 out_sb[:, :, :]).then_inc(out_stored, 16)
                if ffn and n == 0:
                    load_wide(PIECES - 1, g, u)
                if front and n == 9:
                    sp.wait_ge(stack_loaded, reached(16 * STACK_LOADS * f))
                    sp.sem_inc(apart, 1)
                    sp.wait_ge(q_hi_done, reached(f + 1))
                    sp.sem_inc(apart, 1)
                    sp.dma_start(q_hi_d.rearrange("r q t -> q r t"), q_hi[:, :].bitcast(F32)).then_inc(scratch_written, 16)
                    sp.wait_ge(k_hi_done, reached(f + 1))
                    sp.sem_inc(apart, 1)
                    sp.dma_start(k_hi_d.rearrange("r q t -> q r t"), k_hi[:, :].bitcast(F32)).then_inc(scratch_written, 16)
                    sp.wait_ge(q_lo_done, reached(f + 1))
                    sp.sem_inc(apart, 1)
                    sp.dma_start(q_lo_d.rearrange("r q t -> q r t"), q_lo[:, :].bitcast(F32)).then_inc(scratch_written, 16)
                    sp.wait_ge(k_lo_done, reached(f + 1))
                    sp.sem_inc(apart, 1)
                    sp.dma_start(k_lo_d.rearrange("r q t -> q r t"), k_lo[:, :].bitcast(F32)).then_inc(scratch_written, 16)
                if front and n == 11:
                    sp.wait_ge(scratch_written, reached(64 * (f + 1)))
                    sp.sem_inc(apart, 1)
                    sp.wait_ge(scores_ready, reached(SEQS * QUADS * f))
                    sp.sem_inc(apart, 1)
                    sp.wait_ge(zeroed, 1)
                    sp.sem_inc(apart, 1)
                    for part, (qs, ks) in enumerate(((q_hi_d, k_hi_d), (q_hi_d, k_lo_d), (q_lo_d, k_hi_d))):
                        for pair in range(2):
                            r = part * 32 + pair * 16
                            sp.dma_start(q_stack[r:r + 16, :, pair, :].bitcast(F32), qs[16 * pair:16 * pair + 16]).then_inc(stack_loaded, 16)
                            for half in range(2):
                                row = 16 * pair + 8 * half
                                rows = ks[row:row + 8].rearrange("r q (c t) -> r (q c) t", t=CHUNK)
                                sp.dma_start(k_stack[r + 8 * half:r + 8 * half + 8, :, :, half, :].bitcast(F32)
                                             .rearrange("r q c t -> r (q c) t"),
                                             rows
                                             ).then_inc(stack_loaded, 16)
                if mid and n == 15:
                    for p in range(PIECES):
                        sp.wait_ge(wide_loaded[p], reached(32 * m))
                        sp.sem_inc(apart, 1)
                    sp.wait_ge(weightT_copied, reached(m + 1))
                    sp.sem_inc(apart, 1)
                    sp.dma_start(weight_d[1 - u], weightT[:, :]).then_inc(weight_written, 16)
                if mid and n == 16:
                    for p in range(PIECES - 1):
                        load_wide(p, m, 1 - u)

            def load_wide(p, g, u):
                sp.wait_ge(weight_written, reached(16 * (g + 1)))
                sp.sem_inc(apart, 1)
                if isinstance(g, int) and g == 0:
                    sp.wait_ge(split_done, 4)
                    sp.sem_inc(apart, 1)
                sp.wait_ge(hidden_done, reached(ROUTED * (g - 1) + PIECE * (p + 1)))
                sp.sem_inc(apart, 1)
                src = weight_d[u].rearrange("(b e) t -> e b t", e=2)
                for e in range(2):
                    sp.dma_start(weight_wide[64 * e:64 * e + 64, PIECE * p:PIECE * (p + 1), :],
                                 src[e, PIECE * p:PIECE * (p + 1), :].partition_broadcast(64)
                                 ).then_inc(wide_loaded[p], 16)

            schedule(slot, sp)
            sp.wait_ge(out_stored, 16 * GROUPS)

        @block.tensor
        def _(pe):
            def mm(out, lhsT, rhs, start=True, stop=True, **k):
                return nc.tensor.matmul(out, lhsT, rhs, start=start, stop=stop, **k)

            pe.wait_ge(w_attn_loaded, 32)
            pe.wait_ge(setup_chain, 1)
            mm(mid_banks[0][:, 0:DIM], bv_wide[:, :], woT).then_inc(bias_mm, 1)

            def up(n, g, u):
                if n == 0:
                    pe.wait_ge(x1_hi_done, reached(g + 1))
                    pe.wait_ge(x1_lo_done, reached(g + 1))
                if isinstance(g, int) and g == 0 and n == 0:
                    pe.wait_ge(split_done, 4)
                cols = slice(128 * n, 128 * n + 128)
                for k, hi, lo, ready in ((2 * n, gate_hi, gate_lo, g_ready), (2 * n + 1, up_hi, up_lo, u_ready)):
                    before = k - 3
                    if before < 0:
                        before = {0: 2 * BLOCKS - 1, 1: 2 * BLOCKS - 3, 2: 2 * BLOCKS - 2}[k]
                        base = BLOCKS * (g - 1)
                    else:
                        base = BLOCKS * g
                    if before % 2:
                        pe.wait_ge(gated_done, reached(base + before // 2 + 1))
                    else:
                        pe.wait_ge(silu_done, reached(base + before // 2 + 1))
                    out = up_banks[k % 3][:, :]
                    mm(out, hi[:, cols], x1_hi[u][:, :], stop=False)
                    mm(out, hi[:, cols], x1_lo[u][:, :], start=False, stop=False)
                    mm(out, lo[:, cols], x1_hi[u][:, :], start=False).then_inc(ready, 1)

            def down(n, g):
                if n == 0:
                    pe.wait_ge(gated_done, reached(BLOCKS * g + 1))
                    pe.wait_ge(y_copied, reached(g))
                    if isinstance(g, int) and g == 0:
                        pe.wait_ge(down_loaded, 16)
                else:
                    pe.wait_ge(hidden_done, reached(ROUTED * g + n))
                mm(y_bank[:, :], down_w[:, 128 * n:128 * n + 128], hidden[n % 3][:, :],
                   start=n == 0, stop=n == BLOCKS - 1).then_inc(down_done, 1)

            def scores(m, i):
                b, q = divmod(i, QUADS)
                if i == 0:
                    pe.wait_ge(stack_loaded, reached(16 * STACK_LOADS * (m + 1)))
                    pe.wait_ge(gate_exp, reached(m))
                elif i == 1:
                    pe.wait_ge(weightT_copied, reached(m))
                else:
                    pe.wait_ge(probs_done, reached(SEQS * QUADS * m + i - 1))
                for c in range(CHUNKS):
                    t = slice(b * SEQ + c * CHUNK, b * SEQ + (c + 1) * CHUNK)
                    last = mm(mid_banks[i % 2][:, 128 * c:128 * c + 128],
                              k_stack[:, q, b * CHUNKS + c, :, :].rearrange("r h t -> r (h t)"),
                              q_stack[:, q, :, t])
                last.then_inc(scores_ready, 1)

            def between_chunks(m, b):
                if b == 0:
                    pe.wait_ge(k_exp, reached(m + 1))
                    pe.wait_ge(q_exp, reached(m + 1))
                    pe.wait_ge(kv_masked, reached(SEQS * (m + 1)))
                for c in range(CHUNKS - 1):
                    t = slice(b * SEQ + (c + 1) * CHUNK, (b + 1) * SEQ)
                    mm(o_bank[:, t], kv_blocks[:, b, c, :], qT[:, t], start=c == 0, stop=False,
                       skip_group_check=True)

            def within_chunks(m, b):
                pe.wait_ge(probs_done, reached(SEQS * QUADS * m + QUADS * (b + 1)))
                for c in range(CHUNKS):
                    t = slice(b * SEQ + c * CHUNK, b * SEQ + (c + 1) * CHUNK)
                    for pair in range(2):
                        for q in range(QUADS):
                            v = v_pair[:, (b * CHUNKS + c) * QUADS + q, 2 * pair:2 * pair + 2, :]
                            last = mm(o_bank[32 * q:32 * q + 32, t], v, probs[:, b, q, c, pair, :],
                                      start=False, stop=pair == 1, skip_group_check=True)
                if b == SEQS - 1:
                    last.then_inc(o_ready, 1)

            def slot(n, g, u, ffn, mid, front, tail):
                m, f = g + 1, g + 2
                if ffn:
                    up(n, g, u)
                if tail and n < 2:
                    down(BLOCKS - 2 + n, g - 1)
                if ffn and n >= LAG:
                    down(n - LAG, g)
                if tail and n == 3:
                    t = g - 1
                    pe.wait_ge(kv_masked, reached(SEQS * min(t + 3, GROUPS) if isinstance(t, int) else SEQS * (t + 3)))
                    pe.wait_ge(y_copied, reached(t + 1))
                    for i in range(TILES):
                        last = nc.tensor.transpose(work_bank[:, 128 * i:128 * i + 128],
                                                   yT[:, 128 * i:128 * i + 128], ident)
                    last.then_inc(y_turned, 1)
                if mid and n < 4:
                    if isinstance(m, int) and m == 0 and n == 0:
                        pe.wait_ge(bias_done, 1)
                    scores(m, 2 * n)
                    scores(m, 2 * n + 1)
                if mid and n == 2:
                    between_chunks(m, 0)
                if mid and n == 3:
                    within_chunks(m, 0)
                if mid and n == 4:
                    between_chunks(m, 1)
                    pe.wait_ge(qk_sum_done, reached(m + 1))
                    pe.wait_ge(probs_done, reached(SEQS * QUADS * m + 7))
                    for i in range(TILES):
                        last = mm(mid_banks[0][:, HEADS * i:HEADS * i + HEADS],
                                  k_sum[:, 128 * i:128 * i + 128], head_ones)
                    last.then_inc(den_ready, 1)
                if mid and n == 5:
                    within_chunks(m, 1)
                if mid and n == 6:
                    pe.wait_ge(inv_widened, reached(m + 1))
                    pe.wait_ge(probs_done, reached(SEQS * QUADS * (m + 1)))
                    for i in range(TILES):
                        wide = inv_wide[:, HEADS * i:HEADS * (i + 1), :].rearrange("p h d -> p (h d)")
                        last = nc.tensor.transpose(mid_banks[1][:, 128 * i:128 * i + 128], wide, ident)
                    last.then_inc(inv_turned, 1)
                if front and n == 7:
                    pe.wait_ge(resid2_done, reached(f - 1))
                    pe.wait_ge(kv_masked, reached(SEQS * f))
                    pe.wait_ge(xT_loaded, reached(16 * (f + 1)))
                    mm(work_bank[:, :], wqT, xT[:, :]).then_inc(q_proj, 1)
                if mid and n == 8:
                    pe.wait_ge(attn_done, reached(m + 1))
                    pe.wait_ge(inv_done, reached(m + 1))
                    for i in range(TILES):
                        last = mm(mid_banks[0][:, 128 * i:128 * i + 128], attnT[:, 128 * i:128 * i + 128], woT)
                    last.then_inc(proj_ready, 1)
                if front and n == 8:
                    pe.wait_ge(attn_done, reached(f))
                    mm(o_bank[:, :], wkT, xT[:, :]).then_inc(k_proj, 1)
                if front and n in (9, 10):
                    b = n - 9
                    if b == 0:
                        pe.wait_ge(q_exp, reached(f + 1))
                    else:
                        pe.wait_ge(v_masked, reached(SEQS * f + 1))
                    for c in range(CHUNKS):
                        x = xT[:, b * SEQ + c * CHUNK:b * SEQ + (c + 1) * CHUNK]
                        for half in range(2):
                            last = mm(work_bank[64 * half:64 * half + 64, 128 * c:128 * c + 128], x, wvT)
                    last.then_inc(v_proj, 1)
                if mid and n == 11:
                    pe.wait_ge(x1_done, reached(m + 1))
                    pe.wait_ge(inv_copied, reached(m + 1))
                    for i in range(TILES):
                        last = nc.tensor.transpose(mid_banks[1][:, 128 * i:128 * i + 128],
                                                   x1[1 - u][:, i, :], ident)
                    last.then_inc(x1_turned, 1)
                if mid and n == 12:
                    pe.wait_ge(x1T_copied, reached(m + 1))
                    pe.wait_ge(resid_done, reached(m + 1))
                    for i in range(TILES):
                        last = mm(mid_banks[0][:, EXPERTS * i:EXPERTS * (i + 1)],
                                  x1T[:, 128 * i:128 * i + 128], gate_wT)
                    last.then_inc(gate_ready, 1)
                if front and n in (12, 14):
                    b = (n - 12) // 2
                    if b == 0:
                        pe.wait_ge(v_masked, reached(SEQS * (f + 1)))
                        pe.sem_inc(apart, 1)
                        pe.wait_ge(k_exp, reached(f + 1))
                        pe.sem_inc(apart, 1)
                    else:
                        pe.wait_ge(kv_masked, reached(SEQS * f + 1))
                        pe.sem_inc(apart, 1)
                    for c in range(CHUNKS - 1):
                        k = kT[:, b * SEQ + c * CHUNK:b * SEQ + (c + 1) * CHUNK]
                        last = nc.tensor.transpose(work_bank[0:CHUNK, 128 * c:128 * c + 128], k, ident)
                    last.then_inc(kT_turned, 1)
                if front and n in (13, 15):
                    b = (n - 13) // 2
                    pe.wait_ge(kT_copied, reached(SEQS * f + b + 1))
                    for c in range(CHUNKS - 1):
                        first = (b * CHUNKS + c) * QUADS
                        last = mm(work_bank[:, 128 * c:128 * c + 128], k_twice[:, c, :],
                                  v_pair[:, first:first + QUADS, 0:4:3, :])
                    last.then_inc(kv_ready, 1)
                if mid and n == 15:
                    pe.wait_ge(weight_done, reached(m + 1))
                    pe.wait_ge(x1_hi_done, reached(m + 1))
                    for i in range(TILES):
                        last = nc.tensor.transpose(mid_banks[1][0:EXPERTS, 128 * i:128 * i + 128],
                                                   weight[:, EXPERTS * i:EXPERTS * (i + 1)], ident)
                    last.then_inc(weight_turned, 1)

            pe.wait_ge(const_loaded, 48)
            schedule(slot, pe)

        @block.scalar
        def _(act):
            act.wait_ge(w_attn_loaded, 32)

            def slot(n, g, u, ffn, mid, front, tail):
                m, f = g + 1, g + 2
                if tail and n == 2:
                    t = g - 1
                    act.wait_ge(down_done, reached(BLOCKS * (t + 1)))
                    act.wait_ge(y_turned, reached(t))
                    nc.scalar.activation(yT[:, :], y_bank[:, :], ACT.Copy).then_inc(y_copied, 1)
                if ffn:
                    act.wait_ge(g_ready, reached(BLOCKS * g + n + 1))
                    act.wait_ge(gated_done, reached(BLOCKS * g + n - 1 if n >= 2 else BLOCKS * g - n))
                    nc.scalar.activation(silu[n % 2][:, :], up_banks[2 * n % 3][:, :], ACT.Silu
                                         ).then_inc(silu_done, 1)
                if mid and n == 6:
                    act.wait_ge(inv_turned, reached(m + 1))
                    act.wait_ge(attn_done, reached(m))
                    nc.scalar.activation(inv_denT[:, :], mid_banks[1][:, :], ACT.Copy).then_inc(inv_copied, 1)
                if front and n == 8:
                    act.wait_ge(q_proj, reached(f + 1))
                    act.wait_ge(o_ready, reached(f))
                    act.wait_ge(qk_sum_done, reached(f))
                    act.wait_ge(q_lo_done, reached(f))
                    nc.scalar.activation(qT[:, :], work_bank[:, :], ACT.Exp, bias=attn_cols[:, 0:1]
                                         ).then_inc(q_exp, 1)
                    act.wait_ge(k_proj, reached(f + 1))
                    act.wait_ge(kT_turned, reached(SEQS * f))
                    act.wait_ge(k_scanned, reached(SEQS * f))
                    act.wait_ge(k_lo_done, reached(f))
                    nc.scalar.activation(kT[:, :], o_bank[:, :], ACT.Exp, bias=attn_cols[:, 1:2]
                                         ).then_inc(k_exp, 1)
                    act.wait_ge(scratch_written, reached(64 * f))
                    act.wait_ge(q_exp, reached(f + 1))
                    nc.scalar.activation(q_hi[:, :], qT[:, :], ACT.Copy).then_inc(q_hi_done, 1)
                    act.wait_ge(k_exp, reached(f + 1))
                    nc.scalar.activation(k_hi[:, :], kT[:, :], ACT.Copy).then_inc(k_hi_done, 1)
                if mid and n == 11:
                    act.wait_ge(x1_turned, reached(m + 1))
                    act.wait_ge(gate_ready, reached(m))
                    act.wait_ge(x1_lo_done, reached(m))
                    nc.scalar.activation(x1T[:, :], mid_banks[1][:, :], ACT.Copy).then_inc(x1T_copied, 1)
                    act.wait_ge(u_ready, reached(BLOCKS * (m - 1) + 1))
                    nc.scalar.activation(x1_hi[1 - u][:, :], mid_banks[1][:, :], ACT.Copy
                                         ).then_inc(x1_hi_done, 1)
                if mid and n == 12:
                    act.wait_ge(gate_ready, reached(m + 1))
                    act.wait_ge(weight_done, reached(m))
                    nc.scalar.activation(exp_neg[:, :], mid_banks[0][:, 0:NE], ACT.Exp, scale=-1.0
                                         ).then_inc(gate_exp, 1)
                if front and n in (12, 14):
                    b = (n - 12) // 2
                    act.wait_ge(kT_turned, reached(SEQS * f + b + 1))
                    act.wait_ge(kv_ready, reached(SEQS * f + b))
                    for half in range(2):
                        last = nc.scalar.activation(k_twice[64 * half:64 * half + 64, :, :].rearrange("p c t -> p (c t)"),
                                                    work_bank[0:CHUNK, 0:128 * (CHUNKS - 1)], ACT.Copy)
                    last.then_inc(kT_copied, 1)
                if mid and n == 15:
                    act.wait_ge(weight_turned, reached(m + 1))
                    act.wait_ge(weight_written, reached(16 * m))
                    nc.scalar.activation(weightT[:, :], mid_banks[1][0:EXPERTS, :], ACT.Copy
                                         ).then_inc(weightT_copied, 1)
                if isinstance(g, int) and g == -2 and n == 9:
                    act.wait_ge(up_loaded, 16)
                    for hi, i in ((gate_hi, 0), (up_hi, 1)):
                        nc.scalar.activation(hi[:, :], up_raw[:, BLOCKS * 128 * i:BLOCKS * 128 * (i + 1)], ACT.Copy
                                             ).then_inc(split_done, 1)

            schedule(slot, act)

        @block.vector
        def _(dve):
            V = nc.vector
            dve.wait_ge(w_attn_loaded, 32)
            V.tensor_copy(bv_wide[:, :], attn_cols[:, 2:3].to_broadcast([128, 128])).then_inc(setup_chain, 1)
            V.memset(neg_half[:, :], -0.5).then_inc(setup_chain, 1)
            dve.sem_inc(resid2_done, 1)
            dve.wait_ge(const_loaded, 48)
            dve.wait_ge(bias_mm, 1)
            V.tensor_tensor(row_bias[:, :], mid_banks[0][:, 0:DIM], row_bias[:, :], ALU.add
                            ).then_inc(bias_done, 1)

            NORM_LINKS = 2

            def norm_stats(rows, st, mv, var, chain, base, done):
                for i in range(TILES):
                    last = V.bn_stats(st[:, i, :], rows[:, i, :])
                last.then_inc(chain, 1)
                dve.wait_ge(chain, reached(base + 1))
                dve.sem_inc(apart, 1)
                for i in range(TILES):
                    last = V.bn_aggr(mv[:, i, :], st[:, i, :])
                last.then_inc(chain, 1)
                dve.wait_ge(chain, reached(base + NORM_LINKS))
                V.tensor_scalar(var[:, :], mv[:, :, 1], LN_EPS, None, ALU.add).then_inc(done, 1)

            def normalise(dst, rows, mv, rstd, done):
                for i in range(TILES):
                    last = V.tensor_scalar(dst[:, i, :], rows[:, i, :], mv[:, i, 0:1], rstd[:, i:i + 1],
                                           ALU.subtract, ALU.mult)
                last.then_inc(done, 1)

            ROUTE_LINKS = 17

            def route(m):
                links = [0]

                def link(ins):
                    links[0] += 1
                    ins.then_inc(route_chain, 1)
                    dve.wait_ge(route_chain, reached(ROUTE_LINKS * m + links[0]))
                    dve.sem_inc(apart, 1)

                by_tile = lambda a: a[:, :].rearrange("p (a e) -> p a e", a=TILES)
                by_group = lambda a: a[:, :].rearrange("p (k e) -> p k e", k=NG)
                dve.wait_ge(gate_exp, reached(m + 1))
                link(V.tensor_scalar(exp_neg[:, :], exp_neg[:, :], 1.0, None, ALU.add))
                link(V.reciprocal(score[:, :], exp_neg[:, :]))
                link(V.tensor_tensor(by_tile(choice), by_tile(score),
                                     gate_bias[:, :].unsqueeze(1).to_broadcast([128, TILES, EXPERTS]), ALU.add))
                for k in range(NG):
                    last = V.max(top_of_group[:, k, :], by_group(choice)[:, k, :])
                link(last)
                link(V.tensor_tensor(group_score[:, :], top_of_group[:, :, 0], top_of_group[:, :, 1], ALU.add))
                own = group_score[:, :].unsqueeze(2).to_broadcast([128, NG, EXPERT_GROUPS])
                other = group_score[:, :].rearrange("p (a h) -> p a h", a=TILES).unsqueeze(2).to_broadcast(
                    [128, TILES, EXPERT_GROUPS, EXPERT_GROUPS])
                own4 = own.rearrange("p (a h) k -> p a h k", a=TILES)
                four = lambda a: a[:, :, :].rearrange("p (a h) k -> p a h k", a=TILES)
                V.tensor_tensor(four(greater), other, own4, ALU.is_gt)
                link(V.tensor_tensor(four(equal), other, own4, ALU.is_equal))
                flat = lambda a: a[:, :, :].rearrange("p (a h) k -> p a (h k)", a=TILES)
                link(V.tensor_tensor(flat(equal), flat(equal),
                                     lower.unsqueeze(1).to_broadcast([128, TILES, EXPERT_GROUPS ** 2]), ALU.mult))
                link(V.tensor_tensor(greater[:, :, :], greater[:, :, :], equal[:, :, :], ALU.add))
                link(V.tensor_reduce(group_rank[:, :], greater[:, :, :], AX.X, ALU.add))
                link(V.tensor_scalar(group_rank[:, :], group_rank[:, :], float(TOP_GROUPS), None, ALU.is_lt))
                link(V.tensor_tensor(by_group(masked), by_group(choice),
                                     group_rank[:, :].unsqueeze(2).to_broadcast([128, NG, EXPERTS // EXPERT_GROUPS]),
                                     ALU.mult))
                for i in range(TILES):
                    last = V.max(top_vals[:, i, :], by_tile(masked)[:, i, :])
                link(last)
                for i in range(TILES):
                    last = V.match_replace(out=by_tile(replaced)[:, i, :], in_to_replace=top_vals[:, i, :],
                                           in_values=by_tile(masked)[:, i, :], imm_value=-3.0e38)
                link(last)
                dve.wait_ge(weight_turned, reached(m))
                link(V.scalar_tensor_tensor(weight[:, :], replaced[:, :], -2.0e38, score[:, :], ALU.is_lt, ALU.mult))
                link(V.tensor_reduce(weight_sum[:, :], by_tile(weight), AX.X, ALU.add))
                link(V.tensor_scalar(weight_sum[:, :], weight_sum[:, :], 1e-20, 1.0 / ROUTED_SCALING,
                                     ALU.add, ALU.mult))
                link(V.reciprocal(weight_sum[:, :], weight_sum[:, :]))
                V.tensor_tensor(by_tile(weight), by_tile(weight),
                                weight_sum[:, :].unsqueeze(2).to_broadcast([128, TILES, EXPERTS]), ALU.mult
                                ).then_inc(weight_done, 1)
                assert links[0] == ROUTE_LINKS, links

            def slot(n, g, u, ffn, mid, front, tail):
                m, f = g + 1, g + 2
                if ffn:
                    dve.wait_ge(u_ready, reached(BLOCKS * g + n + 1))
                    dve.wait_ge(silu_done, reached(BLOCKS * g + n + 1))
                    if n == 0:
                        dve.wait_ge(down_done, reached(BLOCKS * g - 1))
                        dst = hidden[0]
                    else:
                        dve.wait_ge(hidden_done, reached(ROUTED * g + (n - 3 if n > 3 else {1: 0, 2: -2, 3: -1}[n])))
                        dst = gated[n % 3]
                    V.tensor_tensor(dst[:, :], up_banks[(2 * n + 1) % 3][:, :], silu[n % 2][:, :], ALU.mult
                                    ).then_inc(gated_done, 1)
                if mid and n < 4:
                    for i in (2 * n, 2 * n + 1):
                        b, q = divmod(i, QUADS)
                        dve.wait_ge(scores_ready, reached(SEQS * QUADS * m + i + 1))
                        if i == 0:
                            dve.wait_ge(o_ready, reached(m))
                        V.tensor_tensor(probs[:, b, q, :, :, :].rearrange("p c j s -> p (c j) s"),
                                        mid_banks[i % 2][:, :].rearrange("p (c s) -> p c s", s=CHUNK),
                                        tri.unsqueeze(1).to_broadcast([128, 2 * CHUNKS, CHUNK]), ALU.mult
                                        ).then_inc(probs_done, 1)
                if tail and n == 3:
                    t = g - 1
                    dve.wait_ge(y_turned, reached(t + 1))
                    dve.wait_ge(out_stored, reached(16 * t))
                    V.tensor_tensor(out_sb[:, :, :].rearrange("p a c -> p (a c)"), work_bank[:, :],
                                    x1[1 - u][:, :, :].rearrange("p a c -> p (a c)"), ALU.add
                                    ).then_inc(resid2_done, 1)
                    dve.wait_ge(resid2_done, reached(t + 2))
                    dve.wait_ge(rstd2_done, reached(t))
                    norm_stats(out_sb, stats2, mean_var2, var2, ln2_chain, NORM_LINKS * t, var2_done)
                    dve.wait_ge(rstd2_done, reached(t + 1))
                    normalise(out_sb, out_sb, mean_var2, rstd2, out_done)
                if mid and n == 4:
                    dve.wait_ge(den_ready, reached(m + 1))
                    V.reciprocal(inv_den[:, :], mid_banks[0][:, 0:TILES * HEADS]).then_inc(inv_done, 1)
                    dve.wait_ge(inv_done, reached(m + 1))
                    dve.wait_ge(inv_turned, reached(m))
                    V.tensor_copy(inv_wide[:, :, :], inv_den[:, :].unsqueeze(2).to_broadcast(
                        [128, TILES * HEADS, HEAD_DIM])).then_inc(inv_widened, 1)
                if mid and n == 7:
                    dve.wait_ge(o_ready, reached(m + 1))
                    dve.wait_ge(inv_copied, reached(m + 1))
                    dve.wait_ge(proj_ready, reached(m))
                    V.tensor_tensor(attnT[:, :], o_bank[:, :], inv_denT[:, :], ALU.mult).then_inc(attn_done, 1)
                if mid and n == 9:
                    dve.wait_ge(proj_ready, reached(m + 1))
                    dve.wait_ge(x_bias_done, reached(m + 1))
                    V.tensor_tensor(resid[:, :, :].rearrange("p a c -> p (a c)"), mid_banks[0][:, :],
                                    resid[:, :, :].rearrange("p a c -> p (a c)"), ALU.add
                                    ).then_inc(resid_done, 1)
                    dve.wait_ge(resid_done, reached(m + 1))
                    dve.wait_ge(rstd1_done, reached(m))
                    norm_stats(resid, stats, mean_var, var1, ln_chain, NORM_LINKS * m, var1_done)
                if front and n in (9, 10):
                    b = n - 9
                    dve.wait_ge(v_proj, reached(SEQS * f + b + 1))
                    if b == 0:
                        dve.wait_ge(zeroed, 3)
                        dve.wait_ge(kv_ready, reached(SEQS * f))
                        dve.wait_ge(o_ready, reached(f))
                    first = b * CHUNKS * QUADS
                    V.tensor_tensor(v_pair[:, first:first + CHUNKS * QUADS, 0:4:3, :],
                                    work_bank[:, :].rearrange("p (a j d) -> p a j d", j=2, d=16),
                                    half_mask.unsqueeze(1).unsqueeze(1).to_broadcast([128, CHUNKS * QUADS, 2, 16]),
                                    ALU.mult).then_inc(v_masked, 1)
                if mid and n == 10:
                    dve.wait_ge(rstd1_done, reached(m + 1))
                    dve.wait_ge(resid2_done, reached(m))
                    normalise(x1[1 - u], resid, mean_var, rstd1, x1_done)
                if front and n == 11:
                    dve.wait_ge(k_exp, reached(f + 1))
                    dve.wait_ge(den_ready, reached(f))
                    for b in range(SEQS):
                        k = kT[:, b * SEQ:(b + 1) * SEQ]
                        V.tensor_tensor_scan(k_sum[:, b * SEQ:(b + 1) * SEQ], k, k, 0.0, ALU.add, ALU.bypass
                                             ).then_inc(k_scanned, 1)
                if mid and n == 13:
                    route(m)
                if front and n in (13, 15):
                    b = (n - 13) // 2
                    dve.wait_ge(kv_ready, reached(SEQS * f + b + 1))
                    if b == 0:
                        dve.wait_ge(o_ready, reached(f))
                    V.tensor_tensor(kv_blocks[:, b, :, :],
                                    work_bank[:, 0:128 * (CHUNKS - 1)].rearrange("p (c d) -> p c d", d=128),
                                    block_mask.unsqueeze(1).to_broadcast([128, CHUNKS - 1, 128]), ALU.mult
                                    ).then_inc(kv_masked, 1)

            schedule(slot, dve)

        @block.gpsimd
        def _(pool):
            G = nc.gpsimd
            G.memset(k_stack[:, :, :, :, :].bitcast(F32), 0.0)
            G.memset(q_stack[:, :, :, :].bitcast(F32), 0.0).then_inc(zeroed, 1)
            G.memset(v_pair[:, :, :, :], 0.0).then_inc(zeroed, 2)

            def slot(n, g, u, ffn, mid, front, tail):
                m, f = g + 1, g + 2
                if ffn and n >= 1:
                    if (n - 1) % PIECE == 0:
                        pool.wait_ge(wide_loaded[(n - 1) // PIECE], reached(32 * (g + 1)))
                    pool.wait_ge(gated_done, reached(BLOCKS * g + n + 1))
                    pool.wait_ge(down_done, reached(BLOCKS * g + (n - 2 if n >= 3 else {1: 0, 2: -2}[n])))
                    G.tensor_tensor(hidden[n % 3][:, :], gated[n % 3][:, :], weight_wide[:, n - 1, :], ALU.mult
                                    ).then_inc(hidden_done, 1)
                if mid and n == 5:
                    pool.wait_ge(x_tok_loaded, reached(16 * (m + 1)))
                    pool.wait_ge(x1_done, reached(m))
                    pool.wait_ge(bias_done, 1)
                    G.tensor_tensor(resid[:, :, :], x_tok[:, :, :],
                                    row_bias[:, :].unsqueeze(1).to_broadcast([128, TILES, DIM]), ALU.add
                                    ).then_inc(x_bias_done, 1)
                if tail and n == 3:
                    t = g - 1
                    pool.wait_ge(var2_done, reached(t + 1))
                    pool.wait_ge(out_done, reached(t))
                    G.tensor_tensor(rstd2[:, :], var2[:, :], neg_half[:, :], ALU.pow).then_inc(rstd2_done, 1)
                if front and n == 9:
                    pool.wait_ge(scratch_written, reached(64 * f))
                    pool.wait_ge(q_hi_done, reached(f + 1))
                    G.tensor_tensor(q_lo[:, :], qT[:, :], q_hi[:, :].bitcast(F32), ALU.subtract
                                    ).then_inc(q_lo_done, 1)
                    pool.wait_ge(k_hi_done, reached(f + 1))
                    G.tensor_tensor(k_lo[:, :], kT[:, :], k_hi[:, :].bitcast(F32), ALU.subtract
                                    ).then_inc(k_lo_done, 1)
                if mid and n == 9:
                    pool.wait_ge(setup_chain, 2)
                    pool.wait_ge(var1_done, reached(m + 1))
                    pool.wait_ge(x1_done, reached(m))
                    G.tensor_tensor(rstd1[:, :], var1[:, :], neg_half[:, :], ALU.pow).then_inc(rstd1_done, 1)
                if mid and n == 11:
                    pool.wait_ge(x1T_copied, reached(m + 1))
                    pool.wait_ge(x1_hi_done, reached(m + 1))
                    pool.wait_ge(u_ready, reached(BLOCKS * (m - 1) + 1))
                    G.tensor_tensor(x1_lo[1 - u][:, :], x1T[:, :], x1_hi[1 - u][:, :].bitcast(F32), ALU.subtract
                                    ).then_inc(x1_lo_done, 1)
                if front and n == 12:
                    pool.wait_ge(k_scanned, reached(SEQS * (f + 1)))
                    pool.wait_ge(q_exp, reached(f + 1))
                    G.tensor_tensor(k_sum[:, :], k_sum[:, :], qT[:, :], ALU.mult).then_inc(qk_sum_done, 1)
                if isinstance(g, int) and g == -2 and n == 13:
                    pool.wait_ge(split_done, 2)
                    for i, (lo, hi) in enumerate(((gate_lo, gate_hi), (up_lo, up_hi))):
                        G.tensor_tensor(lo[:, :], up_raw[:, BLOCKS * 128 * i:BLOCKS * 128 * (i + 1)],
                                        hi[:, :].bitcast(F32), ALU.subtract).then_inc(split_done, 1)

            schedule(slot, pool)


def _constants():
    import numpy as np
    p = np.arange(128)[:, None]
    parts = {
        "ident": p == np.arange(128)[None, :],
        "block": p // HEAD_DIM == np.arange(128)[None, :] // HEAD_DIM,
        "tri": p % CHUNK <= np.arange(CHUNK)[None, :],
        "half": p // CHUNK == np.arange(16)[None, :] // HEAD_DIM,
        "ones": p // HEAD_DIM == np.arange(HEADS)[None, :],
        "lower": (np.arange(16)[None, :] % 4 < np.arange(16)[None, :] // 4) & (p >= 0),
    }
    return np.concatenate([parts[n] for n in CONST_COLS], axis=1).astype(np.float32)


def kernel(**inputs):
    import numpy as np
    import concourse.bacc as bacc
    from concourse.bass_utils import run_bass_kernel_spmd

    a = {k: np.asarray(v) for k, v in inputs.items()}
    x = a["L0_attn_x"].reshape(TOKENS, DIM)

    def up_layout(routed, shared):
        return np.concatenate([shared, routed.reshape(EXPERTS * INTER, DIM)], axis=0).T

    def down_layout(routed, shared):
        rows = np.concatenate([shared.T, routed.transpose(0, 2, 1).reshape(EXPERTS * INTER, DIM)], axis=0)
        return rows.reshape(BLOCKS, 128, DIM).transpose(1, 0, 2).reshape(128, BLOCKS * DIM)

    arrays = {
        "xT_in": x.T,
        "x_in": x,
        "attn_w_in": np.concatenate([a["L0_attn_Wq"].T, a["L0_attn_Wk"].T, a["L0_attn_Wv"].T, a["L0_attn_Wo"].T,
                                     a["L0_ffn_gate_w"].T], axis=1),
        "attn_cols_in": np.stack([a["L0_attn_bq"], a["L0_attn_bk"], a["L0_attn_bv"]], axis=1),
        "bo_in": a["L0_attn_bo"],
        "gate_bias_in": a["L0_ffn_gate_bias"],
        "up_in": np.concatenate([up_layout(a["L0_ffn_expert_gate"], a["L0_ffn_shared_gate"]),
                                 up_layout(a["L0_ffn_expert_up"], a["L0_ffn_shared_up"])], axis=1),
        "down_in": down_layout(a["L0_ffn_expert_down"], a["L0_ffn_shared_down"]),
        "const_in": _constants(),
    }
    arrays = {k: np.ascontiguousarray(v) for k, v in arrays.items()}
    nc = bacc.Bacc("TRN2", target_bir_lowering=False, num_devices=1)
    F32 = mybir.dt.float32
    args = [nc.dram_tensor(k, v.shape, F32, kind="ExternalInput").ap() for k, v in arrays.items()]
    out = nc.dram_tensor("out_dram", (TOKENS, DIM), F32, kind="ExternalOutput").ap()
    attention_moe_kernel(nc, *args, out)
    r = run_bass_kernel_spmd(nc, [arrays], core_ids=[0])
    return r.results[0]["out_dram"].reshape(TOKENS // SEQ, SEQ, DIM)
```

```python
import concourse.bass as bass
from concourse import mybir
from contextlib import ExitStack

TOKENS, DIM = 4096, 128
SEQ, HEADS, HEAD_DIM = 256, 16, 8
EXPERTS, INTER = 32, 64
EXPERT_GROUPS, TOP_K, TOP_GROUPS = 4, 8, 2
ROUTED_SCALING = 2.5
LN_EPS = 1e-5

GROUP = 512
GROUPS = TOKENS // GROUP
TILES = GROUP // 128
SEQS = GROUP // SEQ
CHUNK = 64
CHUNKS = SEQ // CHUNK
QUADS = HEADS // 4
PARTS = 3
STACK = PARTS * 32
BLOCKS = EXPERTS * INTER // 128 + 1
ROUTED = BLOCKS - 1
PIECES = 4
PIECE = ROUTED // PIECES
SLOTS = BLOCKS
HEAD_SLOTS = 5
LAG = 3
POOL_LOWS = (9, 10, 11)
VECTOR_LOWS = BLOCKS - len(POOL_LOWS)
STACK_LOADS = 2 + 4

CONST_COLS = {"ident": 128, "block": 128, "tri": 64, "ones": 16, "lower": 16}


def attention_moe_kernel(nc, xT_d, x_d, attn_w_d, attn_cols_d, bo_d, gate_bias_d,
                         up_d, down_d, const_d, out_d):
    F32, F32R = mybir.dt.float32, mybir.dt.float32r
    ALU = mybir.AluOpType
    ACT = mybir.ActivationFunctionType
    AX = mybir.AxisListType

    ctx = ExitStack()
    with ctx:
        def sb(name, shape, dt=F32):
            return ctx.enter_context(nc.sbuf_tensor(name, shape, dt))

        def sem(name):
            return ctx.enter_context(nc.semaphore(name))

        const = sb("const", [128, sum(CONST_COLS.values())])
        at, views = 0, {}
        for name, n in CONST_COLS.items():
            views[name] = const[:, at:at + n]
            at += n
        ident, block_mask, tri = views["ident"], views["block"], views["tri"]
        head_ones, lower = views["ones"], views["lower"]
        attn_w = sb("attn_w", [128, 4 * DIM + EXPERTS])
        wqT, wkT, wvT, woT = (attn_w[:, i * DIM:(i + 1) * DIM] for i in range(4))
        gate_wT = attn_w[:, 4 * DIM:4 * DIM + EXPERTS]
        attn_cols = sb("attn_cols", [128, 3])
        row_bias = sb("row_bias", [128, DIM])
        gate_bias = sb("gate_bias", [128, EXPERTS])
        bv_wide = sb("bv_wide", [128, 128])
        gate_hi = sb("gate_hi", [128, BLOCKS * 128], F32R)
        gate_lo = sb("gate_lo", [128, BLOCKS * 128], F32R)
        up_hi = sb("up_hi", [128, BLOCKS * 128], F32R)
        up_lo = sb("up_lo", [128, BLOCKS * 128], F32R)
        down_hi = sb("down_hi", [128, BLOCKS * 128], F32R)
        down_lo = sb("down_lo", [128, BLOCKS * 128], F32R)
        neg_half = sb("neg_half", [128, TILES])

        xT = sb("xT", [128, GROUP])
        qT, kT = sb("qT", [128, GROUP]), sb("kT", [128, GROUP])
        q_hi, q_lo = sb("q_hi", [128, GROUP], F32R), sb("q_lo", [128, GROUP], F32R)
        k_hi, k_lo = sb("k_hi", [128, GROUP], F32R), sb("k_lo", [128, GROUP], F32R)
        k_sum = sb("k_sum", [128, GROUP])
        k_stack = sb("k_stack", [STACK, QUADS, SEQS * CHUNKS, 2, CHUNK], F32R)
        q_stack = sb("q_stack", [STACK, QUADS, 2, GROUP], F32R)
        v_pair = sb("v_pair", [128, SEQS * CHUNKS * QUADS, 4, 16])
        k_twice = sb("k_twice", [128, CHUNKS - 1, 128])
        kv_blocks = sb("kv_blocks", [128, SEQS, CHUNKS - 1, 128])

        probs = sb("probs", [128, SEQS, QUADS, CHUNKS, 2, CHUNK])
        inv_den = sb("inv_den", [128, TILES * HEADS])
        inv_wide = sb("inv_wide", [128, TILES * HEADS, HEAD_DIM])
        inv_denT = sb("inv_denT", [128, GROUP])
        attnT = sb("attnT", [128, GROUP])
        x_tok = sb("x_tok", [128, TILES, DIM])
        resid = sb("resid", [128, TILES, DIM])
        stats = sb("stats", [128, TILES, 6])
        mean_var = sb("mean_var", [128, TILES, 2])
        var1, rstd1 = sb("var1", [128, TILES]), sb("rstd1", [128, TILES])
        x1 = [sb(f"x1_{u}", [128, TILES, DIM]) for u in range(2)]
        x1T = sb("x1T", [128, GROUP])
        x1_hi = [sb(f"x1_hi{u}", [128, GROUP], F32R) for u in range(2)]
        x1_lo = [sb(f"x1_lo{u}", [128, GROUP], F32R) for u in range(2)]
        NE = TILES * EXPERTS
        NG = TILES * EXPERT_GROUPS
        exp_neg = sb("exp_neg", [128, NE])
        score = sb("score", [128, NE])
        choice = sb("choice", [128, NE])
        top_of_group = sb("top_of_group", [128, NG, 8])
        group_score = sb("group_score", [128, NG])
        ahead = sb("ahead", [128, NG, 2, EXPERT_GROUPS])
        group_rank = sb("group_rank", [128, NG])
        masked = sb("masked", [128, NE])
        top_vals = sb("top_vals", [128, TILES, 8])
        replaced = sb("replaced", [128, NE])
        weight_sum = sb("weight_sum", [128, TILES])
        weight = sb("weight", [128, NE])
        weightT = sb("weightT", [EXPERTS, GROUP])

        weight_wide = sb("weight_wide", [128, 2 * PIECE, GROUP])
        units = [sb(f"units{i}", [128, GROUP]) for i in range(3)]
        hidden_hi = [sb(f"hidden_hi{i}", [128, GROUP], F32R) for i in range(3)]
        hidden_lo = [sb(f"hidden_lo{i}", [128, GROUP], F32R) for i in range(3)]
        yT = sb("yT", [128, GROUP])
        stats2 = sb("stats2", [128, TILES, 6])
        mean_var2 = sb("mean_var2", [128, TILES, 2])
        var2, rstd2 = sb("var2", [128, TILES]), sb("rstd2", [128, TILES])
        out_sb = sb("out_sb", [128, TILES, DIM])
        gate_raw = down_raw = weight_wide[:, :, :].rearrange("p b t -> p (b t)")[:, 0:BLOCKS * 128]
        up_raw = probs[:, :, :, :, :, :].rearrange("p b q c j s -> p (b q c j s)")[:, 0:BLOCKS * 128]

        q_parts_d = nc.dram_tensor("q_parts_d", (4, PARTS, HEAD_DIM, QUADS, GROUP), F32).ap()
        k_parts_d = nc.dram_tensor("k_parts_d", (4, PARTS, HEAD_DIM, QUADS, GROUP), F32).ap()
        weight_d = nc.dram_tensor("weight_d", (2, EXPERTS, GROUP), F32).ap()

        banks = [ctx.enter_context(nc.psum_tensor(f"bank{i}", [128, 512], F32)) for i in range(8)]
        up_banks = banks[0:3]
        y_bank = banks[3]
        mid_banks = banks[4:6]
        work_bank = banks[6]
        o_bank = banks[7]

        apart, const_loaded, zeroed, w_attn_loaded = (sem(n) for n in ("apart", "const_loaded", "zeroed", "w_attn_loaded"))
        up_loaded, down_loaded, gate_split, up_split, down_split, setup_chain = (
            sem(n) for n in ("up_loaded", "down_loaded", "gate_split", "up_split", "down_split", "setup_chain"))
        bias_mm, bias_done, xT_loaded, q_proj = (sem(n) for n in ("bias_mm", "bias_done", "xT_loaded", "q_proj"))
        q_exp, q_hi_done, q_lo_done, k_proj = (sem(n) for n in ("q_exp", "q_hi_done", "q_lo_done", "k_proj"))
        k_exp, k_hi_done, k_lo_done, k_written = (sem(n) for n in ("k_exp", "k_hi_done", "k_lo_done", "k_written"))
        q_written = sem("q_written")
        stack_loaded, v_proj, v_copied, kT_turned = (sem(n) for n in ("stack_loaded", "v_proj", "v_copied", "kT_turned"))
        kT_copied, kv_ready, kv_masked, k_scanned = (sem(n) for n in ("kT_copied", "kv_ready", "kv_masked", "k_scanned"))
        qk_sum_done, scores_ready, probs_done, o_ready = (sem(n) for n in ("qk_sum_done", "scores_ready", "probs_done", "o_ready"))
        den_ready, inv_done, inv_widened, inv_turned = (sem(n) for n in ("den_ready", "inv_done", "inv_widened", "inv_turned"))
        inv_copied, attn_done, proj_ready, x_tok_loaded = (sem(n) for n in ("inv_copied", "attn_done", "proj_ready", "x_tok_loaded"))
        x_bias_done, resid_done, ln_chain, var1_done = (sem(n) for n in ("x_bias_done", "resid_done", "ln_chain", "var1_done"))
        rstd1_done, x1_done, x1_turned, x1T_copied = (sem(n) for n in ("rstd1_done", "x1_done", "x1_turned", "x1T_copied"))
        x1_hi_done, x1_lo_done, gate_ready, gate_exp = (sem(n) for n in ("x1_hi_done", "x1_lo_done", "gate_ready", "gate_exp"))
        route_chain, weight_done, weight_turned, weightT_copied = (sem(n) for n in ("route_chain", "weight_done", "weight_turned", "weightT_copied"))
        weight_written, g_ready, u_ready, silu_done = (sem(n) for n in ("weight_written", "g_ready", "u_ready", "silu_done"))
        gated_done, hidden_done, down_done, y_copied = (sem(n) for n in ("gated_done", "hidden_done", "down_done", "y_copied"))
        hidden_hi_done, hidden_lo_done, pool_lo_done = (sem(n) for n in ("hidden_hi_done", "hidden_lo_done", "pool_lo_done"))
        y_turned, resid2_done, ln2_chain, var2_done = (sem(n) for n in ("y_turned", "resid2_done", "ln2_chain", "var2_done"))
        rstd2_done, out_done, out_stored = (sem(n) for n in ("rstd2_done", "out_done", "out_stored"))
        wide_loaded = [sem(f"wide_loaded{p}") for p in range(PIECES)]

        def reached(count):
            return max(count, 0) if isinstance(count, int) else count

        def vector_lows(n):
            return n + 1 - sum(i <= n for i in POOL_LOWS)


        def schedule(slot, eng):
            def run(slots, g, u, **what):
                for n in slots:
                    slot(n, g, u, **what)
            every, head, rest = range(SLOTS), range(HEAD_SLOTS), range(HEAD_SLOTS, SLOTS)
            run(every, -2, 0, ffn=False, mid=False, front=True, tail=False)
            run(every, -1, 1, ffn=False, mid=True, front=True, tail=False)
            run(head, 0, 0, ffn=True, mid=True, front=True, tail=False)
            with eng.Fori(0, (GROUPS - 2) // 2) as pair:
                for u in range(2):
                    g = pair * 2 + u
                    run(rest, g, u, ffn=True, mid=True, front=True, tail=False)
                    run(head, g + 1, 1 - u, ffn=True, mid=True, front=True, tail=True)
            last = GROUPS - 1
            run(rest, last - 1, 0, ffn=True, mid=True, front=False, tail=False)
            run(head, last, 1, ffn=True, mid=False, front=False, tail=True)
            run(rest, last, 1, ffn=True, mid=False, front=False, tail=False)
            run(head, last + 1, 0, ffn=False, mid=False, front=False, tail=True)

        block = ctx.enter_context(nc.Block())

        @block.sync
        def _(sp):
            sp.dma_start(attn_w[:, :], attn_w_d).then_inc(w_attn_loaded, 16)
            sp.dma_start(attn_cols[:, :], attn_cols_d).then_inc(w_attn_loaded, 16)

            def address(value):
                return value if isinstance(value, int) else sp.snap(value)

            def slot(n, g, u, ffn, mid, front, tail):
                m, f = g + 1, g + 2
                if front and n == 5:
                    at = address(f * GROUP)
                    sp.wait_ge(v_proj, reached(SEQS * f))
                    sp.sem_inc(apart, 1)
                    sp.dma_start(xT[:, :], xT_d[:, bass.ds(at, GROUP)]).then_inc(xT_loaded, 16)
                if mid and n == 5:
                    at = address(m * GROUP)
                    sp.wait_ge(x_bias_done, reached(m))
                    sp.sem_inc(apart, 1)
                    sp.dma_start(x_tok[:, :, :], x_d[bass.ds(at, GROUP), :].rearrange("(a p) c -> p a c", p=128)
                                 ).then_inc(x_tok_loaded, 16)
                if isinstance(g, int) and g == -2 and n == 5:
                    sp.dma_start(const[:, :], const_d).then_inc(const_loaded, 16)
                    sp.dma_start(row_bias[:, :], bo_d.partition_broadcast(128)).then_inc(const_loaded, 16)
                    sp.dma_start(gate_bias[:, :], gate_bias_d.partition_broadcast(128)).then_inc(const_loaded, 16)
                    sp.dma_start(gate_raw, up_d[:, 0:BLOCKS * 128]).then_inc(up_loaded, 16)
                    sp.dma_start(up_raw, up_d[:, BLOCKS * 128:2 * BLOCKS * 128]).then_inc(up_loaded, 16)
                if isinstance(g, int) and g == -2 and n == 16:
                    sp.wait_ge(gate_split, 2)
                    sp.dma_start(down_raw, down_d).then_inc(down_loaded, 16)
                if tail and n == 4:
                    t = g - 1
                    at = address(t * GROUP)
                    sp.wait_ge(out_done, reached(t + 1))
                    sp.sem_inc(apart, 1)
                    sp.dma_start(out_d[bass.ds(at, GROUP), :].rearrange("(a p) c -> p a c", p=128),
                                 out_sb[:, :, :]).then_inc(out_stored, 16)
                if front and n == 8:
                    sp.wait_ge(stack_loaded, reached(16 * STACK_LOADS * f))
                    sp.sem_inc(apart, 1)
                    sp.wait_ge(k_hi_done, reached(f + 1))
                    sp.sem_inc(apart, 1)
                    for part in (1, 2):
                        sp.dma_start(k_parts_d[:, part].rearrange("h r q t -> h (r q) t"), k_hi[:, :].bitcast(F32)
                                     ).then_inc(k_written, 16)
                    sp.wait_ge(k_lo_done, reached(f + 1))
                    sp.sem_inc(apart, 1)
                    sp.dma_start(k_parts_d[:, 0].rearrange("h r q t -> h (r q) t"), k_lo[:, :].bitcast(F32)
                                 ).then_inc(k_written, 16)
                    sp.wait_ge(q_hi_done, reached(f + 1))
                    sp.sem_inc(apart, 1)
                    for part in (0, 1):
                        sp.dma_start(q_parts_d[:, part].rearrange("h r q t -> h (r q) t"), q_hi[:, :].bitcast(F32)
                                     ).then_inc(q_written, 16)
                    sp.wait_ge(q_lo_done, reached(f + 1))
                    sp.sem_inc(apart, 1)
                    sp.dma_start(q_parts_d[:, 2].rearrange("h r q t -> h (r q) t"), q_lo[:, :].bitcast(F32)
                                 ).then_inc(q_written, 16)
                if ffn and n in (5, 9):
                    load_wide(2 + (n - 5) // 4, g, u)
                if front and n == 9:
                    sp.wait_ge(k_written, reached(16 * PARTS * (f + 1)))
                    sp.sem_inc(apart, 1)
                    sp.wait_ge(scores_ready, reached(SEQS * QUADS * f))
                    sp.sem_inc(apart, 1)
                    sp.wait_ge(zeroed, 1)
                    sp.sem_inc(apart, 1)
                    rows = PARTS * HEAD_DIM
                    for h in range(4):
                        sp.dma_start(k_stack[rows * h:rows * (h + 1), :, :, h % 2, :].bitcast(F32)
                                     .rearrange("r q c t -> r (q c) t"),
                                     k_parts_d[h].rearrange("p r q (c t) -> (p r) (q c) t", t=CHUNK)
                                     ).then_inc(stack_loaded, 16)
                    sp.wait_ge(q_written, reached(16 * PARTS * (f + 1)))
                    sp.sem_inc(apart, 1)
                    for pair in range(2):
                        sp.dma_start(q_stack[2 * rows * pair:2 * rows * (pair + 1), :, pair, :].bitcast(F32),
                                     q_parts_d[2 * pair:2 * pair + 2].rearrange("h p r q t -> (h p r) q t")
                                     ).then_inc(stack_loaded, 16)
                if mid and n == 14:
                    for p in range(PIECES):
                        sp.wait_ge(wide_loaded[p], reached(32 * m))
                        sp.sem_inc(apart, 1)
                    sp.wait_ge(weightT_copied, reached(m + 1))
                    sp.sem_inc(apart, 1)
                    sp.dma_start(weight_d[1 - u], weightT[:, :]).then_inc(weight_written, 16)
                if mid and n == 16:
                    for p in range(2):
                        load_wide(p, m, 1 - u)

            def load_wide(p, g, u):
                sp.wait_ge(weight_written, reached(16 * (g + 1)))
                sp.sem_inc(apart, 1)
                if isinstance(g, int) and g == 0:
                    sp.wait_ge(down_split, 2)
                    sp.sem_inc(apart, 1)
                sp.wait_ge(hidden_done, reached(ROUTED * g + PIECE * (p - 1)))
                sp.sem_inc(apart, 1)
                src = weight_d[u].rearrange("(b e) t -> e b t", e=2)
                for e in range(2):
                    sp.dma_start(weight_wide[64 * e:64 * e + 64, PIECE * (p % 2):PIECE * (p % 2 + 1), :],
                                 src[e, PIECE * p:PIECE * (p + 1), :].partition_broadcast(64)
                                 ).then_inc(wide_loaded[p], 16)

            schedule(slot, sp)
            sp.wait_ge(out_stored, 16 * GROUPS)

        @block.tensor
        def _(pe):
            def mm(out, lhsT, rhs, start=True, stop=True, **k):
                return nc.tensor.matmul(out, lhsT, rhs, start=start, stop=stop, **k)

            pe.wait_ge(w_attn_loaded, 32)
            pe.wait_ge(setup_chain, 1)
            mm(mid_banks[0][:, 0:DIM], bv_wide[:, :], woT).then_inc(bias_mm, 1)

            def up(n, g, u):
                if n == 0:
                    pe.wait_ge(x1_hi_done, reached(g + 1))
                    pe.wait_ge(x1_lo_done, reached(g + 1))
                if isinstance(g, int) and g == 0 and n == 0:
                    pe.wait_ge(gate_split, 2)
                    pe.wait_ge(up_split, 2)
                    pe.wait_ge(down_split, 2)
                cols = slice(128 * n, 128 * n + 128)
                for k, hi, lo, ready in ((2 * n, gate_hi, gate_lo, g_ready), (2 * n + 1, up_hi, up_lo, u_ready)):
                    before = k - 3
                    if before < 0:
                        before = {0: 2 * BLOCKS - 1, 1: 2 * BLOCKS - 3, 2: 2 * BLOCKS - 2}[k]
                        base = BLOCKS * (g - 1)
                    else:
                        base = BLOCKS * g
                    if before % 2:
                        pe.wait_ge(gated_done, reached(base + before // 2 + 1))
                    else:
                        pe.wait_ge(silu_done, reached(base + before // 2 + 1))
                    out = up_banks[k % 3][:, :]
                    mm(out, hi[:, cols], x1_hi[u][:, :], stop=False)
                    mm(out, hi[:, cols], x1_lo[u][:, :], start=False, stop=False)
                    mm(out, lo[:, cols], x1_hi[u][:, :], start=False).then_inc(ready, 1)

            def down(n, g):
                if n in POOL_LOWS:
                    pe.wait_ge(pool_lo_done, reached(len(POOL_LOWS) * g + POOL_LOWS.index(n) + 1))
                else:
                    pe.wait_ge(hidden_lo_done, reached(VECTOR_LOWS * g + vector_lows(n)))
                if n == 0:
                    pe.wait_ge(y_copied, reached(g))
                cols, h = slice(128 * n, 128 * n + 128), n % 3
                mm(y_bank[:, :], down_hi[:, cols], hidden_hi[h][:, :], start=n == 0, stop=False)
                mm(y_bank[:, :], down_hi[:, cols], hidden_lo[h][:, :], start=False, stop=False)
                mm(y_bank[:, :], down_lo[:, cols], hidden_hi[h][:, :], start=False, stop=n == BLOCKS - 1
                   ).then_inc(down_done, 1)

            def scores(m, i):
                b, q = divmod(i, QUADS)
                if i == 0:
                    pe.wait_ge(stack_loaded, reached(16 * STACK_LOADS * (m + 1)))
                    pe.wait_ge(gate_exp, reached(m))
                elif i == 1:
                    pe.wait_ge(weightT_copied, reached(m))
                else:
                    pe.wait_ge(probs_done, reached(SEQS * QUADS * m + i - 1))
                for c in range(CHUNKS):
                    t = slice(b * SEQ + c * CHUNK, b * SEQ + (c + 1) * CHUNK)
                    last = mm(mid_banks[i % 2][:, 128 * c:128 * c + 128],
                              k_stack[:, q, b * CHUNKS + c, :, :].rearrange("r h t -> r (h t)"),
                              q_stack[:, q, :, t])
                last.then_inc(scores_ready, 1)

            def between_chunks(m, b):
                if b == 0:
                    pe.wait_ge(k_exp, reached(m + 1))
                    pe.wait_ge(q_exp, reached(m + 1))
                    pe.wait_ge(kv_masked, reached(SEQS * (m + 1)))
                for c in range(CHUNKS - 1):
                    t = slice(b * SEQ + (c + 1) * CHUNK, (b + 1) * SEQ)
                    mm(o_bank[:, t], kv_blocks[:, b, c, :], qT[:, t], start=c == 0, stop=False,
                       skip_group_check=True)

            def within_chunks(m, b):
                pe.wait_ge(probs_done, reached(SEQS * QUADS * m + QUADS * (b + 1)))
                for c in range(CHUNKS):
                    t = slice(b * SEQ + c * CHUNK, b * SEQ + (c + 1) * CHUNK)
                    for pair in range(2):
                        for q in range(QUADS):
                            v = v_pair[:, (b * CHUNKS + c) * QUADS + q, 2 * pair:2 * pair + 2, :]
                            last = mm(o_bank[32 * q:32 * q + 32, t], v, probs[:, b, q, c, pair, :],
                                      start=False, stop=pair == 1, skip_group_check=True)
                if b == SEQS - 1:
                    last.then_inc(o_ready, 1)

            def slot(n, g, u, ffn, mid, front, tail):
                m, f = g + 1, g + 2
                if tail and n == 0:
                    down(BLOCKS - LAG, g - 1)
                if ffn:
                    up(n, g, u)
                if tail and 0 < n < LAG:
                    down(BLOCKS - LAG + n, g - 1)
                if mid and n == 10:
                    pe.wait_ge(x1T_copied, reached(m + 1))
                    pe.wait_ge(resid_done, reached(m + 1))
                    for i in range(TILES):
                        last = mm(mid_banks[0][:, EXPERTS * i:EXPERTS * (i + 1)],
                                  x1T[:, 128 * i:128 * i + 128], gate_wT)
                    last.then_inc(gate_ready, 1)
                if ffn and n >= LAG:
                    down(n - LAG, g)
                if tail and n == 3:
                    t = g - 1
                    pe.wait_ge(kv_masked, reached(SEQS * min(t + 3, GROUPS) if isinstance(t, int) else SEQS * (t + 3)))
                    pe.wait_ge(y_copied, reached(t + 1))
                    for i in range(TILES):
                        last = nc.tensor.transpose(work_bank[:, 128 * i:128 * i + 128],
                                                   yT[:, 128 * i:128 * i + 128], ident)
                    last.then_inc(y_turned, 1)
                if mid and n < 4:
                    if isinstance(m, int) and m == 0 and n == 0:
                        pe.wait_ge(bias_done, 1)
                    scores(m, 2 * n)
                    scores(m, 2 * n + 1)
                if mid and n == 2:
                    between_chunks(m, 0)
                if mid and n == 3:
                    within_chunks(m, 0)
                if mid and n == 4:
                    between_chunks(m, 1)
                    pe.wait_ge(qk_sum_done, reached(m + 1))
                    pe.wait_ge(probs_done, reached(SEQS * QUADS * m + 7))
                    for i in range(TILES):
                        last = mm(mid_banks[0][:, HEADS * i:HEADS * i + HEADS],
                                  k_sum[:, 128 * i:128 * i + 128], head_ones)
                    last.then_inc(den_ready, 1)
                if mid and n == 5:
                    within_chunks(m, 1)
                if mid and n == 5:
                    pe.wait_ge(inv_widened, reached(m + 1))
                    pe.wait_ge(probs_done, reached(SEQS * QUADS * (m + 1)))
                    for i in range(TILES):
                        wide = inv_wide[:, HEADS * i:HEADS * (i + 1), :].rearrange("p h d -> p (h d)")
                        last = nc.tensor.transpose(mid_banks[1][:, 128 * i:128 * i + 128], wide, ident)
                    last.then_inc(inv_turned, 1)
                if front and n == 7:
                    pe.wait_ge(resid2_done, reached(f - 1))
                    pe.wait_ge(kv_masked, reached(SEQS * f))
                    pe.wait_ge(xT_loaded, reached(16 * (f + 1)))
                    mm(work_bank[:, :], wqT, xT[:, :]).then_inc(q_proj, 1)
                if mid and n == 7:
                    pe.wait_ge(attn_done, reached(m + 1))
                    pe.wait_ge(inv_done, reached(m + 1))
                    for i in range(TILES):
                        last = mm(mid_banks[0][:, 128 * i:128 * i + 128], attnT[:, 128 * i:128 * i + 128], woT)
                    last.then_inc(proj_ready, 1)
                if front and n == 7:
                    pe.wait_ge(attn_done, reached(f))
                    mm(o_bank[:, :], wkT, xT[:, :]).then_inc(k_proj, 1)
                if mid and n == 9:
                    pe.wait_ge(x1_done, reached(m + 1))
                    pe.wait_ge(inv_copied, reached(m + 1))
                    for i in range(TILES):
                        last = nc.tensor.transpose(mid_banks[1][:, 128 * i:128 * i + 128],
                                                   x1[1 - u][:, i, :], ident)
                    last.then_inc(x1_turned, 1)
                if front and n in (8, 9):
                    b = n - 8
                    if b == 0:
                        pe.wait_ge(q_exp, reached(f + 1))
                    else:
                        pe.wait_ge(v_copied, reached(SEQS * f + 1))
                    for c in range(CHUNKS):
                        x = xT[:, b * SEQ + c * CHUNK:b * SEQ + (c + 1) * CHUNK]
                        for half in range(2):
                            last = mm(work_bank[64 * half:64 * half + 64, 128 * c:128 * c + 128], x, wvT)
                    last.then_inc(v_proj, 1)
                if front and n in (11, 13):
                    b = (n - 11) // 2
                    if isinstance(g, int) and g == -2 and b == 0:
                        pe.wait_ge(const_loaded, 48)
                    if b == 0:
                        pe.wait_ge(v_copied, reached(SEQS * (f + 1)))
                        pe.sem_inc(apart, 1)
                        pe.wait_ge(k_exp, reached(f + 1))
                        pe.sem_inc(apart, 1)
                    else:
                        pe.wait_ge(kv_masked, reached(SEQS * f + 1))
                        pe.sem_inc(apart, 1)
                    for c in range(CHUNKS - 1):
                        k = kT[:, b * SEQ + c * CHUNK:b * SEQ + (c + 1) * CHUNK]
                        last = nc.tensor.transpose(work_bank[0:CHUNK, 128 * c:128 * c + 128], k, ident)
                    last.then_inc(kT_turned, 1)
                if front and n in (12, 14):
                    b = (n - 12) // 2
                    pe.wait_ge(kT_copied, reached(SEQS * f + b + 1))
                    for c in range(CHUNKS - 1):
                        first = (b * CHUNKS + c) * QUADS
                        last = mm(work_bank[:, 128 * c:128 * c + 128], k_twice[:, c, :],
                                  v_pair[:, first:first + QUADS, 0:4:3, :])
                    last.then_inc(kv_ready, 1)
                if mid and n == 14:
                    pe.wait_ge(weight_done, reached(m + 1))
                    pe.wait_ge(x1_hi_done, reached(m + 1))
                    for i in range(TILES):
                        last = nc.tensor.transpose(mid_banks[1][0:EXPERTS, 128 * i:128 * i + 128],
                                                   weight[:, EXPERTS * i:EXPERTS * (i + 1)], ident)
                    last.then_inc(weight_turned, 1)

            schedule(slot, pe)

        @block.scalar
        def _(act):
            act.wait_ge(w_attn_loaded, 32)

            def high_part(n, g):
                if n == 0:
                    act.wait_ge(gated_done, reached(BLOCKS * g + 1))
                else:
                    act.wait_ge(hidden_done, reached(ROUTED * g + n))
                act.wait_ge(down_done, reached(BLOCKS * g + (n - 2 if n >= 3 else {0: -1, 1: 0, 2: -2}[n])))
                nc.scalar.activation(hidden_hi[n % 3][:, :], units[n % 3][:, :], ACT.Copy
                                     ).then_inc(hidden_hi_done, 1)

            def slot(n, g, u, ffn, mid, front, tail):
                m, f = g + 1, g + 2
                if tail and n == 3:
                    t = g - 1
                    act.wait_ge(down_done, reached(BLOCKS * (t + 1)))
                    act.wait_ge(y_turned, reached(t))
                    nc.scalar.activation(yT[:, :], y_bank[:, :], ACT.Copy).then_inc(y_copied, 1)
                if ffn:
                    act.wait_ge(g_ready, reached(BLOCKS * g + n + 1))
                    before = n - 3 if n >= 3 else {0: 15, 1: 16, 2: 14}[n]
                    in_group = g if n >= 3 else g - 1
                    if before in POOL_LOWS:
                        act.wait_ge(pool_lo_done, reached(len(POOL_LOWS) * in_group + POOL_LOWS.index(before) + 1))
                    else:
                        act.wait_ge(hidden_lo_done, reached(VECTOR_LOWS * in_group + vector_lows(before)))
                    nc.scalar.activation(units[n % 3][:, :], up_banks[2 * n % 3][:, :], ACT.Silu
                                         ).then_inc(silu_done, 1)
                if mid and n == 5:
                    act.wait_ge(inv_turned, reached(m + 1))
                    act.wait_ge(attn_done, reached(m))
                    nc.scalar.activation(inv_denT[:, :], mid_banks[1][:, :], ACT.Copy).then_inc(inv_copied, 1)
                if front and n == 7:
                    act.wait_ge(q_proj, reached(f + 1))
                    act.wait_ge(o_ready, reached(f))
                    act.wait_ge(qk_sum_done, reached(f))
                    act.wait_ge(q_lo_done, reached(f))
                    nc.scalar.activation(qT[:, :], work_bank[:, :], ACT.Exp, bias=attn_cols[:, 0:1]
                                         ).then_inc(q_exp, 1)
                    act.wait_ge(k_proj, reached(f + 1))
                    act.wait_ge(kT_turned, reached(SEQS * f))
                    act.wait_ge(k_scanned, reached(SEQS * f))
                    act.wait_ge(k_lo_done, reached(f))
                    nc.scalar.activation(kT[:, :], o_bank[:, :], ACT.Exp, bias=attn_cols[:, 1:2]
                                         ).then_inc(k_exp, 1)
                if front and n == 8:
                    act.wait_ge(k_written, reached(16 * PARTS * f))
                    act.wait_ge(k_exp, reached(f + 1))
                    nc.scalar.activation(k_hi[:, :], kT[:, :], ACT.Copy).then_inc(k_hi_done, 1)
                    act.wait_ge(q_written, reached(16 * PARTS * f))
                    act.wait_ge(q_exp, reached(f + 1))
                    nc.scalar.activation(q_hi[:, :], qT[:, :], ACT.Copy).then_inc(q_hi_done, 1)
                if mid and n == 9:
                    act.wait_ge(x1_turned, reached(m + 1))
                    act.wait_ge(gate_ready, reached(m))
                    act.wait_ge(x1_lo_done, reached(m))
                    nc.scalar.activation(x1T[:, :], mid_banks[1][:, :], ACT.Copy).then_inc(x1T_copied, 1)
                    act.wait_ge(u_ready, reached(BLOCKS * (m - 1) + 1))
                    nc.scalar.activation(x1_hi[1 - u][:, :], mid_banks[1][:, :], ACT.Copy
                                         ).then_inc(x1_hi_done, 1)
                if front and n in (8, 9):
                    b = n - 8
                    act.wait_ge(v_proj, reached(SEQS * f + b + 1))
                    if b == 0:
                        act.wait_ge(zeroed, 3)
                        act.wait_ge(kv_ready, reached(SEQS * f))
                        act.wait_ge(o_ready, reached(f))
                    first = b * CHUNKS * QUADS
                    for half in range(2):
                        rows, dims = slice(64 * half, 64 * half + 64), slice(HEAD_DIM * half, HEAD_DIM * (half + 1))
                        last = nc.scalar.activation(
                            v_pair[rows, first:first + CHUNKS * QUADS, 0:4:3, dims],
                            work_bank[rows, :].rearrange("p (a j d) -> p a j d", j=2, d=16)[:, :, :, dims], ACT.Copy)
                    last.then_inc(v_copied, 1)
                if mid and n == 10:
                    act.wait_ge(gate_ready, reached(m + 1))
                    act.wait_ge(weight_done, reached(m))
                    nc.scalar.activation(exp_neg[:, :], mid_banks[0][:, 0:NE], ACT.Exp, scale=-1.0
                                         ).then_inc(gate_exp, 1)
                if front and n in (11, 13):
                    b = (n - 11) // 2
                    act.wait_ge(kT_turned, reached(SEQS * f + b + 1))
                    act.wait_ge(kv_ready, reached(SEQS * f + b))
                    for half in range(2):
                        last = nc.scalar.activation(k_twice[64 * half:64 * half + 64, :, :].rearrange("p c t -> p (c t)"),
                                                    work_bank[0:CHUNK, 0:128 * (CHUNKS - 1)], ACT.Copy)
                    last.then_inc(kT_copied, 1)
                if mid and n == 14:
                    act.wait_ge(weight_turned, reached(m + 1))
                    act.wait_ge(weight_written, reached(16 * m))
                    nc.scalar.activation(weightT[:, :], mid_banks[1][0:EXPERTS, :], ACT.Copy
                                         ).then_inc(weightT_copied, 1)
                if tail and n == 0:
                    high_part(BLOCKS - 1, g - 1)
                if ffn and n >= 1:
                    high_part(n - 1, g)
                if isinstance(g, int) and g == -2 and n == 9:
                    act.wait_ge(up_loaded, 32)
                    nc.scalar.activation(gate_hi[:, :], gate_raw, ACT.Copy).then_inc(gate_split, 1)
                if isinstance(g, int) and g == -2 and n == 12:
                    nc.scalar.activation(up_hi[:, :], up_raw, ACT.Copy).then_inc(up_split, 1)
                if isinstance(g, int) and g == -1 and n == 4:
                    act.wait_ge(down_loaded, 16)
                    nc.scalar.activation(down_hi[:, :], down_raw, ACT.Copy).then_inc(down_split, 1)

            schedule(slot, act)

        @block.vector
        def _(dve):
            V = nc.vector
            dve.wait_ge(w_attn_loaded, 32)
            V.tensor_copy(bv_wide[:, :], attn_cols[:, 2:3].to_broadcast([128, 128])).then_inc(setup_chain, 1)
            V.memset(neg_half[:, :], -0.5).then_inc(setup_chain, 1)
            dve.sem_inc(resid2_done, 1)
            dve.wait_ge(const_loaded, 48)
            dve.wait_ge(bias_mm, 1)
            V.tensor_tensor(row_bias[:, :], mid_banks[0][:, 0:DIM], row_bias[:, :], ALU.add
                            ).then_inc(bias_done, 1)

            def low_part(n, g):
                dve.wait_ge(hidden_hi_done, reached(BLOCKS * g + n + 1))
                V.tensor_tensor(hidden_lo[n % 3][:, :], units[n % 3][:, :],
                                hidden_hi[n % 3][:, :].bitcast(F32), ALU.subtract).then_inc(hidden_lo_done, 1)

            NORM_LINKS = 2

            def norm_stats(rows, st, mv, var, chain, base, done):
                for i in range(TILES):
                    last = V.bn_stats(st[:, i, :], rows[:, i, :])
                last.then_inc(chain, 1)
                dve.wait_ge(chain, reached(base + 1))
                dve.sem_inc(apart, 1)
                for i in range(TILES):
                    last = V.bn_aggr(mv[:, i, :], st[:, i, :])
                last.then_inc(chain, 1)
                dve.wait_ge(chain, reached(base + NORM_LINKS))
                V.tensor_scalar(var[:, :], mv[:, :, 1], LN_EPS, None, ALU.add).then_inc(done, 1)

            def normalise(dst, rows, mv, rstd, done):
                for i in range(TILES):
                    last = V.tensor_scalar(dst[:, i, :], rows[:, i, :], mv[:, i, 0:1], rstd[:, i:i + 1],
                                           ALU.subtract, ALU.mult)
                last.then_inc(done, 1)

            ROUTE_LINKS = 15

            def by_tile(a):
                return a[:, :].rearrange("p (a e) -> p a e", a=TILES)

            def by_group(a):
                return a[:, :].rearrange("p (k e) -> p k e", k=NG)

            def linked(ins, m, number):
                ins.then_inc(route_chain, 1)
                dve.wait_ge(route_chain, reached(ROUTE_LINKS * m + number))
                dve.sem_inc(apart, 1)

            def expert_scores(m):
                dve.wait_ge(gate_exp, reached(m + 1))
                linked(V.tensor_scalar(exp_neg[:, :], exp_neg[:, :], 1.0, None, ALU.add), m, 1)
                linked(V.reciprocal(score[:, :], exp_neg[:, :]), m, 2)
                linked(V.tensor_tensor(by_tile(choice), by_tile(score),
                                       gate_bias[:, :].unsqueeze(1).to_broadcast([128, TILES, EXPERTS]), ALU.add), m, 3)

            def group_tops(m):
                for k in range(NG):
                    last = V.max(top_of_group[:, k, :], by_group(choice)[:, k, :])
                linked(last, m, 4)

            def masked_experts(m):
                linked(V.tensor_tensor(group_score[:, :], top_of_group[:, :, 0], top_of_group[:, :, 1], ALU.add), m, 5)
                own = group_score[:, :].unsqueeze(2).to_broadcast([128, NG, EXPERT_GROUPS])
                other = group_score[:, :].rearrange("p (a h) -> p a h", a=TILES).unsqueeze(2).to_broadcast(
                    [128, TILES, EXPERT_GROUPS, EXPERT_GROUPS])
                own4 = own.rearrange("p (a h) k -> p a h k", a=TILES)
                four = lambda a: a.rearrange("p (a h) k -> p a h k", a=TILES)
                greater, equal = ahead[:, :, 0, :], ahead[:, :, 1, :]
                V.tensor_tensor(four(greater), other, own4, ALU.is_gt)
                linked(V.tensor_tensor(four(equal), other, own4, ALU.is_equal), m, 6)
                linked(V.tensor_tensor(four(equal), four(equal),
                                       lower.rearrange("p (h k) -> p h k", k=EXPERT_GROUPS).unsqueeze(1).to_broadcast(
                                           [128, TILES, EXPERT_GROUPS, EXPERT_GROUPS]), ALU.mult), m, 7)
                linked(V.tensor_reduce(group_rank[:, :], ahead[:, :, :, :].rearrange("p k t h -> p k (t h)"),
                                       AX.X, ALU.add), m, 8)
                linked(V.scalar_tensor_tensor(
                    by_group(masked), group_rank[:, :].unsqueeze(2).to_broadcast([128, NG, EXPERTS // EXPERT_GROUPS]),
                    float(TOP_GROUPS), by_group(choice), ALU.is_lt, ALU.mult), m, 9)

            def expert_weights(m):
                for i in range(TILES):
                    last = V.max(top_vals[:, i, :], by_tile(masked)[:, i, :])
                linked(last, m, 10)
                for i in range(TILES):
                    last = V.match_replace(out=by_tile(replaced)[:, i, :], in_to_replace=top_vals[:, i, :],
                                           in_values=by_tile(masked)[:, i, :], imm_value=-3.0e38)
                linked(last, m, 11)
                dve.wait_ge(weight_turned, reached(m))
                linked(V.scalar_tensor_tensor(weight[:, :], replaced[:, :], -2.0e38, score[:, :], ALU.is_lt, ALU.mult), m, 12)
                linked(V.tensor_reduce(weight_sum[:, :], by_tile(weight), AX.X, ALU.add), m, 13)
                linked(V.tensor_scalar(weight_sum[:, :], weight_sum[:, :], 1e-20, 1.0 / ROUTED_SCALING,
                                       ALU.add, ALU.mult), m, 14)
                linked(V.reciprocal(weight_sum[:, :], weight_sum[:, :]), m, 15)
                V.tensor_tensor(by_tile(weight), by_tile(weight),
                                weight_sum[:, :].unsqueeze(2).to_broadcast([128, TILES, EXPERTS]), ALU.mult
                                ).then_inc(weight_done, 1)

            def slot(n, g, u, ffn, mid, front, tail):
                m, f = g + 1, g + 2
                if ffn:
                    dve.wait_ge(u_ready, reached(BLOCKS * g + n + 1))
                    dve.wait_ge(silu_done, reached(BLOCKS * g + n + 1))
                    V.tensor_tensor(units[n % 3][:, :], up_banks[(2 * n + 1) % 3][:, :], units[n % 3][:, :], ALU.mult
                                    ).then_inc(gated_done, 1)
                if mid and n < 4:
                    for i in (2 * n, 2 * n + 1):
                        b, q = divmod(i, QUADS)
                        dve.wait_ge(scores_ready, reached(SEQS * QUADS * m + i + 1))
                        if i == 0:
                            dve.wait_ge(o_ready, reached(m))
                        if i == 0 and isinstance(m, int) and m == 0:
                            dve.wait_ge(up_split, 2)
                        V.tensor_tensor(probs[:, b, q, :, :, :].rearrange("p c j s -> p (c j) s"),
                                        mid_banks[i % 2][:, :].rearrange("p (c s) -> p c s", s=CHUNK),
                                        tri.unsqueeze(1).to_broadcast([128, 2 * CHUNKS, CHUNK]), ALU.mult
                                        ).then_inc(probs_done, 1)
                if tail and n == 3:
                    t = g - 1
                    dve.wait_ge(y_turned, reached(t + 1))
                    dve.wait_ge(out_stored, reached(16 * t))
                    V.tensor_tensor(out_sb[:, :, :].rearrange("p a c -> p (a c)"), work_bank[:, :],
                                    x1[1 - u][:, :, :].rearrange("p a c -> p (a c)"), ALU.add
                                    ).then_inc(resid2_done, 1)
                    dve.wait_ge(resid2_done, reached(t + 2))
                    dve.wait_ge(rstd2_done, reached(t))
                    norm_stats(out_sb, stats2, mean_var2, var2, ln2_chain, NORM_LINKS * t, var2_done)
                if mid and n == 4:
                    dve.wait_ge(den_ready, reached(m + 1))
                    V.reciprocal(inv_den[:, :], mid_banks[0][:, 0:TILES * HEADS]).then_inc(inv_done, 1)
                    dve.wait_ge(inv_done, reached(m + 1))
                    dve.wait_ge(inv_turned, reached(m))
                    V.tensor_copy(inv_wide[:, :, :], inv_den[:, :].unsqueeze(2).to_broadcast(
                        [128, TILES * HEADS, HEAD_DIM])).then_inc(inv_widened, 1)
                if tail and n == 4:
                    t = g - 1
                    dve.wait_ge(rstd2_done, reached(t + 1))
                    normalise(out_sb, out_sb, mean_var2, rstd2, out_done)
                if mid and n == 6:
                    dve.wait_ge(o_ready, reached(m + 1))
                    dve.wait_ge(inv_copied, reached(m + 1))
                    dve.wait_ge(proj_ready, reached(m))
                    V.tensor_tensor(attnT[:, :], o_bank[:, :], inv_denT[:, :], ALU.mult).then_inc(attn_done, 1)
                if mid and n == 7:
                    dve.wait_ge(proj_ready, reached(m + 1))
                    dve.wait_ge(x_bias_done, reached(m + 1))
                    V.tensor_tensor(resid[:, :, :].rearrange("p a c -> p (a c)"), mid_banks[0][:, :],
                                    resid[:, :, :].rearrange("p a c -> p (a c)"), ALU.add
                                    ).then_inc(resid_done, 1)
                    dve.wait_ge(resid_done, reached(m + 1))
                    dve.wait_ge(rstd1_done, reached(m))
                    norm_stats(resid, stats, mean_var, var1, ln_chain, NORM_LINKS * m, var1_done)
                if mid and n == 8:
                    dve.wait_ge(rstd1_done, reached(m + 1))
                    dve.wait_ge(resid2_done, reached(m))
                    normalise(x1[1 - u], resid, mean_var, rstd1, x1_done)
                if front and n == 9:
                    dve.wait_ge(k_exp, reached(f + 1))
                    dve.wait_ge(den_ready, reached(f))
                    for b in range(SEQS):
                        k = kT[:, b * SEQ:(b + 1) * SEQ]
                        V.tensor_tensor_scan(k_sum[:, b * SEQ:(b + 1) * SEQ], k, k, 0.0, ALU.add, ALU.bypass
                                             ).then_inc(k_scanned, 1)
                if front and n in (12, 14):
                    b = (n - 12) // 2
                    dve.wait_ge(kv_ready, reached(SEQS * f + b + 1))
                    if b == 0:
                        dve.wait_ge(o_ready, reached(f))
                    V.tensor_tensor(kv_blocks[:, b, :, :],
                                    work_bank[:, 0:128 * (CHUNKS - 1)].rearrange("p (c d) -> p c d", d=128),
                                    block_mask.unsqueeze(1).to_broadcast([128, CHUNKS - 1, 128]), ALU.mult
                                    ).then_inc(kv_masked, 1)
                if mid and n == 10:
                    expert_scores(m)
                    group_tops(m)
                if mid and n == 11:
                    masked_experts(m)
                if mid and n == 12:
                    expert_weights(m)

                if tail and n == 0:
                    low_part(BLOCKS - 1, g - 1)
                if ffn and n >= 1 and n - 1 not in POOL_LOWS:
                    low_part(n - 1, g)
                if isinstance(g, int) and g == -2 and n == 10:
                    dve.wait_ge(gate_split, 1)
                    V.tensor_tensor(gate_lo[:, :], gate_raw, gate_hi[:, :].bitcast(F32), ALU.subtract
                                    ).then_inc(gate_split, 1)
                if isinstance(g, int) and g == -2 and n == 13:
                    dve.wait_ge(up_split, 1)
                    V.tensor_tensor(up_lo[:, :], up_raw, up_hi[:, :].bitcast(F32), ALU.subtract
                                    ).then_inc(up_split, 1)

            schedule(slot, dve)

        @block.gpsimd
        def _(pool):
            G = nc.gpsimd
            G.memset(k_stack[:, :, :, :, :].bitcast(F32), 0.0)
            G.memset(q_stack[:, :, :, :].bitcast(F32), 0.0).then_inc(zeroed, 1)
            G.memset(v_pair[:, :, :, :], 0.0).then_inc(zeroed, 2)

            def slot(n, g, u, ffn, mid, front, tail):
                m, f = g + 1, g + 2
                if ffn and n >= 1:
                    if (n - 1) % PIECE == 0:
                        pool.wait_ge(wide_loaded[(n - 1) // PIECE], reached(32 * (g + 1)))
                    pool.wait_ge(gated_done, reached(BLOCKS * g + n + 1))
                    G.tensor_tensor(units[n % 3][:, :], units[n % 3][:, :],
                                    weight_wide[:, (n - 1) % (2 * PIECE), :], ALU.mult
                                    ).then_inc(hidden_done, 1)
                if mid and n == 5:
                    pool.wait_ge(x_tok_loaded, reached(16 * (m + 1)))
                    pool.wait_ge(x1_done, reached(m))
                    pool.wait_ge(bias_done, 1)
                    G.tensor_tensor(resid[:, :, :], x_tok[:, :, :],
                                    row_bias[:, :].unsqueeze(1).to_broadcast([128, TILES, DIM]), ALU.add
                                    ).then_inc(x_bias_done, 1)
                if tail and n == 3:
                    t = g - 1
                    pool.wait_ge(var2_done, reached(t + 1))
                    pool.wait_ge(out_done, reached(t))
                    G.tensor_tensor(rstd2[:, :], var2[:, :], neg_half[:, :], ALU.pow).then_inc(rstd2_done, 1)
                if front and n == 8:
                    pool.wait_ge(k_written, reached(16 * PARTS * f))
                    pool.wait_ge(k_hi_done, reached(f + 1))
                    G.tensor_tensor(k_lo[:, :], kT[:, :], k_hi[:, :].bitcast(F32), ALU.subtract
                                    ).then_inc(k_lo_done, 1)
                    pool.wait_ge(q_written, reached(16 * PARTS * f))
                    pool.wait_ge(q_hi_done, reached(f + 1))
                    G.tensor_tensor(q_lo[:, :], qT[:, :], q_hi[:, :].bitcast(F32), ALU.subtract
                                    ).then_inc(q_lo_done, 1)
                if mid and n == 7:
                    pool.wait_ge(setup_chain, 2)
                    pool.wait_ge(var1_done, reached(m + 1))
                    pool.wait_ge(x1_done, reached(m))
                    G.tensor_tensor(rstd1[:, :], var1[:, :], neg_half[:, :], ALU.pow).then_inc(rstd1_done, 1)
                if mid and n == 9:
                    pool.wait_ge(x1T_copied, reached(m + 1))
                    pool.wait_ge(x1_hi_done, reached(m + 1))
                    pool.wait_ge(u_ready, reached(BLOCKS * (m - 1) + 1))
                    G.tensor_tensor(x1_lo[1 - u][:, :], x1T[:, :], x1_hi[1 - u][:, :].bitcast(F32), ALU.subtract
                                    ).then_inc(x1_lo_done, 1)
                if front and n == 15:
                    pool.wait_ge(k_scanned, reached(SEQS * (f + 1)))
                    pool.wait_ge(q_exp, reached(f + 1))
                    G.tensor_tensor(k_sum[:, :], k_sum[:, :], qT[:, :], ALU.mult).then_inc(qk_sum_done, 1)
                if ffn and n - 1 in POOL_LOWS:
                    pool.wait_ge(hidden_hi_done, reached(BLOCKS * g + n))
                    b = (n - 1) % 3
                    G.tensor_tensor(hidden_lo[b][:, :], units[b][:, :], hidden_hi[b][:, :].bitcast(F32), ALU.subtract
                                    ).then_inc(pool_lo_done, 1)
                if isinstance(g, int) and g == -1 and n == 4:
                    pool.wait_ge(down_split, 1)
                    G.tensor_tensor(down_lo[:, :], down_raw, down_hi[:, :].bitcast(F32), ALU.subtract
                                    ).then_inc(down_split, 1)

            schedule(slot, pool)


def _qk_order(rows):
    quads_last = rows.reshape(QUADS, 4, HEAD_DIM, -1).transpose(1, 2, 0, 3)
    return quads_last.reshape(rows.shape)


def _constants():
    import numpy as np
    p = np.arange(128)[:, None]
    head = _qk_order(p[:, 0])[:, None] // HEAD_DIM
    parts = {
        "ident": p == np.arange(128)[None, :],
        "block": head == np.arange(128)[None, :] // HEAD_DIM,
        "tri": p % CHUNK <= np.arange(CHUNK)[None, :],
        "ones": head == np.arange(HEADS)[None, :],
        "lower": (np.arange(16)[None, :] % 4 < np.arange(16)[None, :] // 4) & (p >= 0),
    }
    return np.concatenate([parts[n] for n in CONST_COLS], axis=1).astype(np.float32)


def kernel(**inputs):
    import numpy as np
    import concourse.bacc as bacc
    from concourse.bass_utils import run_bass_kernel_spmd

    a = {k: np.asarray(v) for k, v in inputs.items()}
    x = a["L0_attn_x"].reshape(TOKENS, DIM)

    def up_layout(routed, shared):
        return np.concatenate([shared, routed.reshape(EXPERTS * INTER, DIM)], axis=0).T

    def down_layout(routed, shared):
        rows = np.concatenate([shared.T, routed.transpose(0, 2, 1).reshape(EXPERTS * INTER, DIM)], axis=0)
        return rows.reshape(BLOCKS, 128, DIM).transpose(1, 0, 2).reshape(128, BLOCKS * DIM)

    arrays = {
        "xT_in": x.T,
        "x_in": x,
        "attn_w_in": np.concatenate([_qk_order(a["L0_attn_Wq"]).T, _qk_order(a["L0_attn_Wk"]).T, a["L0_attn_Wv"].T, a["L0_attn_Wo"].T,
                                     a["L0_ffn_gate_w"].T], axis=1),
        "attn_cols_in": np.stack([_qk_order(a["L0_attn_bq"]), _qk_order(a["L0_attn_bk"]), a["L0_attn_bv"]],
                                 axis=1),
        "bo_in": a["L0_attn_bo"],
        "gate_bias_in": a["L0_ffn_gate_bias"],
        "up_in": np.concatenate([up_layout(a["L0_ffn_expert_gate"], a["L0_ffn_shared_gate"]),
                                 up_layout(a["L0_ffn_expert_up"], a["L0_ffn_shared_up"])], axis=1),
        "down_in": down_layout(a["L0_ffn_expert_down"], a["L0_ffn_shared_down"]),
        "const_in": _constants(),
    }
    arrays = {k: np.ascontiguousarray(v) for k, v in arrays.items()}
    nc = bacc.Bacc("TRN2", target_bir_lowering=False, num_devices=1)
    F32 = mybir.dt.float32
    args = [nc.dram_tensor(k, v.shape, F32, kind="ExternalInput").ap() for k, v in arrays.items()]
    out = nc.dram_tensor("out_dram", (TOKENS, DIM), F32, kind="ExternalOutput").ap()
    attention_moe_kernel(nc, *args, out)
    r = run_bass_kernel_spmd(nc, [arrays], core_ids=[0])
    return r.results[0]["out_dram"].reshape(TOKENS // SEQ, SEQ, DIM)
```
